# Optimizing a Trainium2 kernel written in Bass

```python
import numpy as np
import jax
import jax.numpy as jnp

def _softmax(x, axis=-1):
    return jax.nn.softmax(x, axis=axis)

def _gelu(x):
    return jax.nn.gelu(x, approximate=True)

def _silu(x):
    return jax.nn.silu(x)

def _sigmoid(x):
    return jax.nn.sigmoid(x)

def _layernorm(x, axis=-1, eps=1e-05):
    m = jnp.mean(x, axis=axis, keepdims=True)
    v = jnp.var(x, axis=axis, keepdims=True)
    return (x - m) / jnp.sqrt(v + eps)

def _scatter_add(tgt, idx, src, axis=0):
    return tgt.at[idx].add(src)

def _segment_sum(src, seg, n):
    return jax.ops.segment_sum(src, seg, n)
kernel_name = 'mk_adj_preln_d2_adj_r2_1192e4'

def setup_inputs(seed: int=0):
    np.random.seed(seed)
    _w = jnp.asarray

    def _rec_inputs():
        import jax
        import jax.numpy as jnp
        _gk = jax.random.key(seed)
        x = -8.776e-05 + 1 * jax.random.normal(jax.random.fold_in(_gk, 1), (10000, 128), jnp.float32)
        _w = (1.0 + jnp.arange(10000, dtype=jnp.float32)) ** (-0.5)
        _w = _w / _w.mean()
        _pij = jnp.clip(0.0004 * _w[:, None] * _w[None, :], 0.0, 1.0)
        _a = jax.random.uniform(jax.random.fold_in(_gk, 2), (10000, 10000)) < _pij
        _a = jnp.logical_or(_a, jnp.eye(10000, dtype=bool))
        _af = _a.astype(jnp.float32)
        _af = _af * jax.random.uniform(jax.random.fold_in(_gk, 3), (10000, 10000), jnp.float32, 0.05, 1)
        adj = _af
        return (x, adj)
    x, adj = _rec_inputs()

    def _L0_gnn_setup():
        import jax, jax.numpy as jnp
        import numpy as np
        N_USER = 10000
        N_ITEM = 10000
        HID = 128
        key = jax.random.key(seed)
        k1, k2, k3, k4, k5, k6, k7 = jax.random.split(key, 7)
        scale = 1.0 / np.sqrt(HID)
        return {'user_feat': jax.random.normal(k1, (N_USER, HID), dtype=jnp.float32), 'item_feat': jax.random.normal(k2, (N_ITEM, HID), dtype=jnp.float32), 'adj': jax.random.uniform(k3, (N_USER, N_ITEM), dtype=jnp.float32), 'W_item': jax.random.uniform(k4, (HID, HID), dtype=jnp.float32, minval=-scale, maxval=scale), 'b_item': jax.random.uniform(k5, (HID,), dtype=jnp.float32, minval=-scale, maxval=scale), 'W_user': jax.random.uniform(k6, (HID, HID), dtype=jnp.float32, minval=-scale, maxval=scale), 'b_user': jax.random.uniform(k7, (HID,), dtype=jnp.float32, minval=-scale, maxval=scale)}
    _L0_gnn_all = _L0_gnn_setup()
    _L0_gnn_in = {k: v for k, v in _L0_gnn_all.items() if k in ('item_feat', 'W_item', 'b_item', 'W_user', 'b_user')}
    del _L0_gnn_all

    def _L1_gnn_setup():
        import jax, jax.numpy as jnp
        import numpy as np
        N = 4096
        F_IN = 128
        F_OUT = 128
        key = jax.random.key(seed)
        k1, k2, k3, k4 = jax.random.split(key, 4)
        x = jax.random.normal(k1, (N, F_IN), dtype=jnp.float32)
        adj = jax.random.uniform(k2, (N, N), dtype=jnp.float32)
        bound = 1.0 / np.sqrt(F_IN)
        W = jax.random.uniform(k3, (F_OUT, F_IN), minval=-bound, maxval=bound, dtype=jnp.float32)
        b = jax.random.uniform(k4, (F_OUT,), minval=-bound, maxval=bound, dtype=jnp.float32)
        return {'x': x, 'adj': adj, 'W': W, 'b': b}
    _L1_gnn_all = _L1_gnn_setup()
    _L1_gnn_in = {k: v for k, v in _L1_gnn_all.items() if k in ('W', 'b')}
    del _L1_gnn_all
    return {'x': x, 'adj': adj, 'L0_gnn_item_feat': _L0_gnn_in['item_feat'], 'L0_gnn_W_item': _L0_gnn_in['W_item'], 'L0_gnn_b_item': _L0_gnn_in['b_item'], 'L0_gnn_W_user': _L0_gnn_in['W_user'], 'L0_gnn_b_user': _L0_gnn_in['b_user'], 'L1_gnn_W': _L1_gnn_in['W'], 'L1_gnn_b': _L1_gnn_in['b']}

def reference(x, adj, L0_gnn_item_feat, L0_gnn_W_item, L0_gnn_b_item, L0_gnn_W_user, L0_gnn_b_user, L1_gnn_W, L1_gnn_b):
    import jax
    import jax.numpy as jnp

    def _L0_gnn_ref(user_feat, item_feat, adj, W_item, b_item, W_user, b_user):
        import jax, jax.numpy as jnp
        import numpy as np
        N_USER = 10000
        N_ITEM = 10000
        HID = 128
        h = item_feat @ W_item.T + b_item
        b = user_feat @ W_user.T + b_user
        return jax.nn.relu(adj @ h + b)

    def _L1_gnn_ref(x, adj, W, b):
        import jax, jax.numpy as jnp
        import numpy as np
        N = 4096
        F_IN = 128
        F_OUT = 128
        rowsum = adj.sum(axis=1)
        d_inv_sqrt = jnp.power(rowsum, -0.5)
        d_inv_sqrt = jnp.where(jnp.isinf(d_inv_sqrt), 0.0, d_inv_sqrt)
        adj_norm = d_inv_sqrt[:, None] * adj * d_inv_sqrt[None, :]
        h = adj_norm @ x
        return h @ W.T + b
    h = jnp.maximum(_layernorm(x, axis=-1), 0.0)
    x = x + _L0_gnn_ref(h, L0_gnn_item_feat, adj, L0_gnn_W_item, L0_gnn_b_item, L0_gnn_W_user, L0_gnn_b_user)
    h = jnp.maximum(_layernorm(x, axis=-1), 0.0)
    x = x + _L1_gnn_ref(h, adj, L1_gnn_W, L1_gnn_b)
    return x

_drawn_inputs = setup_inputs


def setup_inputs(seed=0):
    import zlib

    import numpy as np

    out = dict(_drawn_inputs(seed))
    spreads = {}
    factors = {}
    for name, (base, spread) in spreads.items():
        noise = np.random.default_rng([zlib.crc32(name.encode()), seed]).standard_normal(out[name].shape)
        drawn = base * np.exp(spread * noise) if base else spread * noise
        out[name] = jnp.asarray(drawn.astype(out[name].dtype))
    for name, factor in factors.items():
        out[name] = (out[name] * factor).astype(out[name].dtype)
    return out
```

```python
import concourse.bass as bass
from concourse import mybir

N, F = 10000, 128
P = 125
C = 4
R = P * C
NB = N // R
K = N // R
HALF = K // 2
RAW, SPLIT, STAGE = 5, 2, 4
EPS = 1e-5

NATIVE = (2, 5, 8, 11, 14, 17)
ON_POOL = (1, 3, 5, 7, 9, 11, 13, 15, 17, 6, 12)
SPLITS = {1: [k for k in range(K) if k not in NATIVE], 2: list(range(K))}
POOL_ACC = sorted(ON_POOL)
DVE_ACC = [k for k in range(K) if k not in ON_POOL]
LINKS1, LINKS2 = 23, 1


def chunks(p, b, k):
    return (p - 1) * NB * K + b * K + k + 1


def splits(p, b, k):
    return (p - 1) * NB * len(SPLITS[1]) + b * len(SPLITS[p]) + sum(j <= k for j in SPLITS[p])


def loads(p, b, k):
    return (p - 1) * NB * K // RAW + b * (K // RAW) + k // RAW + 1


def features(p, k):
    return (p - 1) * len(SPLITS[1]) + sum(j <= k for j in SPLITS[p])


def feature_slot(p, k):
    return (features(p, k) - 1) % STAGE, (features(p, k) - 1) // STAGE + 1


def split_slot(p, k):
    return sum(j < k for j in SPLITS[p]) % SPLIT


def sums(engine, b, k):
    return b * len(engine) + sum(j <= k for j in engine)


def earlier(p, b, k, d, of):
    at = of[p].index(k) - d
    if at >= 0:
        return p, b, of[p][at]
    if isinstance(b, int) and b == 0:
        return None if p == 1 else (1, NB - 1, of[1][at])
    return p, b - 1, of[p][at]


ALL = {1: list(range(K)), 2: list(range(K))}


def gnn_kernel(nc, adj, items, xs, wi, wu, w, bi, bu, bl, out):
    f32, f32r = mybir.dt.float32, mybir.dt.float32r
    ALU, ACT = mybir.AluOpType, mybir.ActivationFunctionType

    x1_dram = nc.dram_tensor("x1_and_d", (NB, P, C * F + C), f32, kind="Internal").ap()
    h2_dram = nc.dram_tensor("scaled_h2", (NB, P, C * F), f32, kind="Internal").ap()

    def sb(name, shape, dt=f32):
        return nc.alloc_sbuf_tensor(name, shape, dt)

    feat_hi = sb("feat_hi", [128, K, C, F], f32r)
    feat_lo = sb("feat_lo", [128, K, C, F], f32r)
    raw = sb("raw", [128, RAW, C, R])
    a_hi = sb("a_hi", [128, SPLIT, C, R], f32r)
    a_lo = sb("a_lo", [128, SPLIT, C, R], f32r)
    item_f32 = sb("item_f32", [128, len(NATIVE), C, F])
    stage = sb("stage", [128, STAGE, C, F])
    acc_dve = sb("acc_dve", [128, 2, R])
    acc_pool = sb("acc_pool", [128, 2, R])
    first_half = sb("first_half", [128, R])
    s_t = sb("s_t", [128, R])
    x_in = sb("x_in", [128, C, F])
    h0 = sb("h0", [128, C, F])
    h0_t = sb("h0_t", [128, R])
    x1d = sb("x1d", [128, C * F + C])
    h2 = sb("h2", [128, C, F])
    h2s = sb("h2s", [128, C, F])
    x1_in = sb("x1_in", [128, C * F + C])
    tmp = sb("tmp", [128, C, F])
    res = sb("res", [128, C, F])
    wi_sb, wu_sb, w_sb = sb("wi_sb", [128, F]), sb("wu_sb", [128, F]), sb("w_sb", [128, F])
    bi_sb, bu_sb, bl_sb = sb("bi_sb", [128, F]), sb("bu_sb", [128, F]), sb("bl_sb", [128, F])
    ident = sb("ident", [128, P])
    ones = sb("ones", [128, 1])
    stats = sb("stats", [128, C, 6])
    diff = sb("diff", [128, C])
    neg_mean = sb("neg_mean", [128, C])
    sums_sb = sb("sums_sb", [128, C])
    nonzero = sb("nonzero", [128, C])
    val = sb("val", [128, 2 * C])
    rec = sb("rec", [128, 2 * C])
    root = sb("root", [128, 2 * C])
    newt = sb("newt", [128, 2 * C])
    rs = sb("rs", [128, 2 * C])
    shift = sb("shift", [128, C])

    bank_a = nc.alloc_psum_tensor("bank_a", [128, 512], f32)
    bank_b = nc.alloc_psum_tensor("bank_b", [128, 512], f32)
    nat = nc.alloc_psum_tensor("nat", [128, 512], f32)
    h0_ps = nc.alloc_psum_tensor("h0_ps", [128, 512], f32)
    sums_ps = nc.alloc_psum_tensor("sums_ps", [128, 512], f32)

    def sem(name):
        return nc.alloc_semaphore(name)

    raw_loaded = [sem(f"raw_loaded{i}") for i in range(RAW)]
    stage_loaded = [sem(f"stage_loaded{i}") for i in range(STAGE)]
    native_loaded, consts_loaded = sem("native_loaded"), sem("consts_loaded")
    x_loaded, x1_loaded = sem("x_loaded"), sem("x1_loaded")
    a_hi_ready, a_lo_ready = sem("a_hi_ready"), sem("a_lo_ready")
    feat_hi_ready, feat_lo_ready = sem("feat_hi_ready"), sem("feat_lo_ready")
    chunk_used = sem("chunk_used")
    summed_dve, summed_pool = sem("summed_dve"), sem("summed_pool")
    first_half_saved, s_ready = sem("first_half_saved"), sem("s_ready")
    row_sums_ready, ident_ready, ones_ready = sem("row_sums_ready"), sem("ident_ready"), sem("ones_ready")
    x_rec, x_root, x_norm = sem("x_rec"), sem("x_root"), sem("x_norm")
    h0_ready, h0_turned, h0_t_ready = sem("h0_ready"), sem("h0_turned"), sem("h0_t_ready")
    nat_ready, nat_used = sem("nat_ready"), sem("nat_used")
    x1_rec, x1_root, x1_norm = sem("x1_rec"), sem("x1_root"), sem("x1_norm")
    h2_ready, h2s_ready, res_ready = sem("h2_ready"), sem("h2s_ready"), sem("res_ready")
    x1_stored, h2_stored, out_stored = sem("x1_stored"), sem("h2_stored"), sem("out_stored")
    dve_link, dve_half, pool_half = sem("dve_link"), sem("dve_half"), sem("pool_half")

    block = nc.Block()
    with block:

        @block.sync
        def _(sp):
            def value(v):
                return v if isinstance(v, int) else sp.to_reg(v)

            def load_chunk(p, b, k):
                old = earlier(p, b, k, RAW, ALL)
                if old:
                    op, ob, ok = old
                    if ok in SPLITS[op]:
                        read, count = a_lo_ready, value(splits(op, ob, ok))
                    else:
                        read, count = chunk_used, value(chunks(op, ob, ok))
                    if op == 1:
                        engine, summed = (DVE_ACC, summed_dve) if ok in DVE_ACC else (POOL_ACC, summed_pool)
                        sum_count = value(sums(engine, ob, ok))
                    sp.wait_ge(read, count)
                    if op == 1:
                        sp.wait_ge(summed, sum_count)
                sp.dma_start(raw[:, k % RAW], adj[b, :, k]).then_inc(raw_loaded[k % RAW], 16)

            def load_features(p, k):
                slot, turn = feature_slot(p, k)
                if features(p, k) > STAGE:
                    sp.wait_ge(feat_lo_ready, features(p, k) - STAGE)
                if p == 2:
                    sp.wait_ge(h2_stored, 16 * (k + 1))
                src = items[k] if p == 1 else h2_dram[k]
                sp.dma_start(stage[0:P, slot], src).then_inc(stage_loaded[slot], 16)

            def store_out(n):
                sp.wait_ge(res_ready, n + 1)
                sp.dma_start(out[n], res[0:P]).then_inc(out_stored, 16)

            def stream(p, b, first=False):
                for k in range(K):
                    last_rows = p == 2 and k == K - 1
                    if first and k in SPLITS[p] and not last_rows:
                        load_features(p, k)
                    load_chunk(p, b, k)
                    if first and last_rows:
                        load_features(p, k)
                    if first and p == 1 and k == 1:
                        for i, kn in enumerate(NATIVE):
                            sp.dma_start(item_f32[0:P, i], items[kn]).then_inc(native_loaded, 16)
                    if k == 12 and p == 2 and not first:
                        store_out(b - 1)

            for p in (1, 2):
                stream(p, 0, first=True)
                with sp.Fori(1, NB) as b:
                    stream(p, b)
            store_out(NB - 1)
            sp.wait_ge(x1_stored, 16 * NB)
            sp.wait_ge(h2_stored, 16 * NB)
            sp.wait_ge(out_stored, 16 * NB)

        @block.gpsimd
        def _(pool):
            nc.gpsimd.memset(ones[:], 1.0).then_inc(ones_ready, 1)
            nc.gpsimd.memset(ident[:], 0.0).then_inc(ident_ready, 1)
            pool.wait_ge(ident_ready, 1)
            nc.gpsimd.affine_select(out=ident[:], in_=ident[:], compare_op=ALU.not_equal, fill=1.0,
                                    base=0, pattern=[[-1, P]], channel_multiplier=1).then_inc(ident_ready, 1)

            def sums_of_block(b, first=False):
                for k in POOL_ACC:
                    part = raw[0:P, k % RAW]
                    pool.wait_ge(raw_loaded[k % RAW], 16 * loads(1, b, k))
                    if k == POOL_ACC[0]:
                        if not first:
                            pool.wait_ge(row_sums_ready, b)
                        nc.gpsimd.tensor_tensor(acc_pool[0:P], part[:, 0:2], part[:, 2:4], ALU.add).then_inc(
                            summed_pool, 1)
                    else:
                        pool.wait_ge(summed_pool, sums(POOL_ACC, b, k) - 1)
                        nc.gpsimd.tensor_tensor(acc_pool[0:P], acc_pool[0:P], part[:, 0:2], ALU.add).then_inc(
                            pool_half, 1)
                        pool.wait_ge(pool_half, b * (len(POOL_ACC) - 1) + POOL_ACC.index(k))
                        nc.gpsimd.tensor_tensor(acc_pool[0:P], acc_pool[0:P], part[:, 2:4], ALU.add).then_inc(
                            summed_pool, 1)

            sums_of_block(0, first=True)
            with pool.Fori(1, NB) as b:
                sums_of_block(b)

        @block.scalar
        def _(act):
            for dst, src in ((wi_sb, wi), (wu_sb, wu), (w_sb, w)):
                act.dma_start(dst[:], src).then_inc(consts_loaded, 16)
            for dst, src in ((bi_sb, bi), (bu_sb, bu), (bl_sb, bl)):
                act.dma_start(dst[0:P], src).then_inc(consts_loaded, 16)

            def split_features(p, k):
                slot, turn = feature_slot(p, k)
                act.wait_ge(stage_loaded[slot], 16 * ((features(p, k) - 1) // STAGE + 1))
                if p == 2:
                    act.wait_ge(chunk_used, chunks(1, NB - 1, k))
                nc.scalar.activation(feat_hi[0:P, k], stage[0:P, slot], ACT.Copy).then_inc(feat_hi_ready, 1)

            def split_chunk(p, b, k):
                act.wait_ge(raw_loaded[k % RAW], 16 * loads(p, b, k))
                old = earlier(p, b, k, SPLIT, SPLITS)
                if old:
                    act.wait_ge(chunk_used, chunks(*old))
                nc.scalar.activation(a_hi[0:P, split_slot(p, k)], raw[0:P, k % RAW], ACT.Copy).then_inc(
                    a_hi_ready, 1)

            def tail1(n, k):
                if k == 2:
                    act.wait_ge(x_rec, n + 1)
                    nc.scalar.activation(root[0:P, 0:C], rec[0:P, 0:C], ACT.Sqrt).then_inc(x_root, 1)
                if k == 4:
                    act.wait_ge(x_norm, n + 1)
                    for c in range(C):
                        last = nc.scalar.activation(h0[0:P, c], x_in[0:P, c], ACT.Relu,
                                                    scale=rs[0:P, c:c + 1], bias=shift[0:P, c:c + 1])
                    last.then_inc(h0_ready, 1)
                if k == 6:
                    act.wait_ge(h0_turned, n + 1)
                    nc.scalar.activation(h0_t[:], h0_ps[:, 0:R], ACT.Copy).then_inc(h0_t_ready, 1)
                if k == 12:
                    act.wait_ge(x1_rec, n + 1)
                    nc.scalar.activation(root[0:P], rec[0:P], ACT.Sqrt).then_inc(x1_root, 1)
                if k == 14:
                    act.wait_ge(x1_norm, n + 1)
                    for c in range(C):
                        last = nc.scalar.activation(h2[0:P, c], x1d[0:P, c * F:(c + 1) * F], ACT.Relu,
                                                    scale=rs[0:P, c:c + 1], bias=shift[0:P, c:c + 1])
                    last.then_inc(h2_ready, 1)
                    act.dma_start(x1_dram[n], x1d[0:P]).then_inc(x1_stored, 16)
                if k == 15:
                    act.wait_ge(h2_ready, n + 1)
                    for c in range(C):
                        last = nc.scalar.activation(h2s[0:P, c], h2[0:P, c], ACT.Copy,
                                                    scale=x1d[0:P, C * F + c:C * F + c + 1])
                    last.then_inc(h2s_ready, 1)
                if k == 16:
                    act.wait_ge(h2s_ready, n + 1)
                    act.dma_start(h2_dram[n], h2s[0:P]).then_inc(h2_stored, 16)
                if k == K - 1:
                    act.wait_ge(h2_stored, 16 * (n + 1))

            def load_rows(p, b, first):
                if p == 1:
                    if not first:
                        act.wait_ge(x1_norm, b)
                    act.dma_start(x_in[0:P], xs[b]).then_inc(x_loaded, 16)
                else:
                    if first:
                        act.wait_ge(x1_stored, 16 * (NB - 1))
                    else:
                        act.wait_ge(res_ready, b)
                    act.dma_start(x1_in[0:P], x1_dram[b]).then_inc(x1_loaded, 16)

            def stream(p, b, first=False):
                for k in range(K):
                    if first and k in SPLITS[p]:
                        split_features(p, k)
                    if k in SPLITS[p]:
                        split_chunk(p, b, k)
                    if k == HALF:
                        act.wait_ge(chunk_used, chunks(p, b, HALF - 1))
                        if not (p == 1 and first):
                            act.wait_ge(s_ready, (p - 1) * NB + b)
                        nc.scalar.activation(first_half[:], bank_a[:, 0:R], ACT.Copy).then_inc(first_half_saved, 1)
                    if p == 1 and not first:
                        tail1(b - 1, k)
                    if p == 2 and first:
                        tail1(NB - 1, k)
                    if k == 16:
                        load_rows(p, b, first)

            for p in (1, 2):
                stream(p, 0, first=True)
                with act.Fori(1, NB) as b:
                    stream(p, b)

        @block.vector
        def _(dve):
            def split_features(p, k):
                slot, turn = feature_slot(p, k)
                dve.wait_ge(feat_hi_ready, features(p, k))
                nc.vector.tensor_tensor(feat_lo[0:P, k], stage[0:P, slot], feat_hi[0:P, k].bitcast(f32),
                                        ALU.subtract).then_inc(feat_lo_ready, 1)

            def split_chunk(p, b, k):
                s = split_slot(p, k)
                dve.wait_ge(a_hi_ready, splits(p, b, k))
                nc.vector.tensor_tensor(a_lo[0:P, s], raw[0:P, k % RAW], a_hi[0:P, s].bitcast(f32),
                                        ALU.subtract).then_inc(a_lo_ready, 1)

            def sum_chunk(b, k, first=False):
                part = raw[0:P, k % RAW]
                dve.wait_ge(raw_loaded[k % RAW], 16 * loads(1, b, k))
                if k == DVE_ACC[0]:
                    if not first:
                        dve.wait_ge(row_sums_ready, b)
                    nc.vector.tensor_tensor(acc_dve[0:P], part[:, 0:2], part[:, 2:4], ALU.add).then_inc(
                        summed_dve, 1)
                else:
                    dve.wait_ge(summed_dve, sums(DVE_ACC, b, k) - 1)
                    nc.vector.tensor_tensor(acc_dve[0:P], acc_dve[0:P], part[:, 0:2], ALU.add).then_inc(
                        dve_half, 1)
                    dve.wait_ge(dve_half, b * (len(DVE_ACC) - 1) + DVE_ACC.index(k))
                    nc.vector.tensor_tensor(acc_dve[0:P], acc_dve[0:P], part[:, 2:4], ALU.add).then_inc(
                        summed_dve, 1)

            links = [0, 0]

            def link(ins):
                links[1] += 1
                ins.then_inc(dve_link, 1)
                dve.wait_ge(dve_link, links[0] + links[1])

            def norm_stats(src):
                for c in range(C):
                    ins = nc.vector.bn_stats(stats[0:P, c], src[c])
                link(ins)
                even, odd = stats[0:P, :, 0:3], stats[0:P, :, 3:6]
                nc.vector.tensor_tensor(diff[0:P], even[:, :, 1], odd[:, :, 1], ALU.subtract)
                nc.vector.tensor_tensor(neg_mean[0:P], even[:, :, 1], odd[:, :, 1], ALU.add)
                link(nc.vector.tensor_tensor(val[0:P, 0:C], even[:, :, 2], odd[:, :, 2], ALU.add))
                nc.vector.tensor_tensor(diff[0:P], diff[0:P], diff[0:P], ALU.mult)
                nc.vector.tensor_scalar(neg_mean[0:P], neg_mean[0:P], -0.5, None, ALU.mult)
                link(nc.vector.tensor_scalar(val[0:P, 0:C], val[0:P, 0:C], 1.0 / F, EPS, ALU.mult, ALU.add))
                link(nc.vector.scalar_tensor_tensor(val[0:P, 0:C], diff[0:P], 0.25, val[0:P, 0:C], ALU.mult, ALU.add))

            def newton(width):
                link(nc.vector.tensor_tensor(newt[0:P, 0:width], root[0:P, 0:width], root[0:P, 0:width], ALU.mult))
                link(nc.vector.tensor_tensor(newt[0:P, 0:width], newt[0:P, 0:width], val[0:P, 0:width], ALU.mult))
                link(nc.vector.tensor_scalar(newt[0:P, 0:width], newt[0:P, 0:width], -0.5, 1.5, ALU.mult, ALU.add))
                link(nc.vector.tensor_tensor(rs[0:P, 0:width], root[0:P, 0:width], newt[0:P, 0:width], ALU.mult))

            def tail1(n, k):
                links[0] = n * LINKS1
                if k == 0:
                    links[1] = 0
                    dve.wait_ge(chunk_used, chunks(1, n, K - 1))
                    dve.wait_ge(first_half_saved, n + 1)
                    nc.vector.tensor_tensor(s_t[:], bank_b[:, 0:R], first_half[:], ALU.add).then_inc(s_ready, 1)
                if k == 1:
                    dve.wait_ge(x_loaded, 16 * (n + 1))
                    norm_stats([x_in[0:P, c] for c in range(C)])
                    nc.vector.reciprocal(rec[0:P, 0:C], val[0:P, 0:C]).then_inc(x_rec, 1)
                if k == 3:
                    dve.wait_ge(x_root, n + 1)
                    newton(C)
                    nc.vector.tensor_tensor(shift[0:P], neg_mean[0:P], rs[0:P, 0:C], ALU.mult).then_inc(x_norm, 1)
                if k == 9:
                    dve.wait_ge(row_sums_ready, n + 1)
                    dve.wait_ge(h0_ready, n + 1)
                    link(nc.vector.tensor_copy(sums_sb[0:P], sums_ps[0:P, 0:C]))
                    dve.wait_ge(nat_ready, n + 1)
                    for c in range(C):
                        ins = nc.vector.scalar_tensor_tensor(tmp[0:P, c], bi_sb[0:P], sums_sb[0:P, c:c + 1],
                                                             nat[0:P, c * F:(c + 1) * F], ALU.mult, ALU.add)
                    ins.then_inc(nat_used, 1)
                    dve.wait_ge(nat_used, n + 1)
                    link(nc.vector.tensor_tensor(tmp[0:P], tmp[0:P], bu_sb[0:P].unsqueeze(1).to_broadcast([P, C, F]),
                                                 ALU.add))
                    link(nc.vector.scalar_tensor_tensor(
                        x1d[0:P, 0:C * F], tmp[0:P].rearrange("p c f -> p (c f)"), 0.0,
                        x_in[0:P].rearrange("p c f -> p (c f)"), ALU.max, ALU.add))
                if k == 11:
                    norm_stats([x1d[0:P, c * F:(c + 1) * F] for c in range(C)])
                    link(nc.vector.tensor_scalar(nonzero[0:P], sums_sb[0:P], 0.0, None, ALU.is_equal))
                    link(nc.vector.tensor_tensor(val[0:P, C:2 * C], sums_sb[0:P], nonzero[0:P], ALU.add))
                    nc.vector.reciprocal(rec[0:P], val[0:P]).then_inc(x1_rec, 1)
                    link(nc.vector.tensor_scalar(nonzero[0:P], nonzero[0:P], -1.0, 1.0, ALU.mult, ALU.add))
                if k == 13:
                    dve.wait_ge(x1_root, n + 1)
                    newton(2 * C)
                    link(nc.vector.tensor_tensor(x1d[0:P, C * F:], rs[0:P, C:2 * C], nonzero[0:P], ALU.mult))
                    nc.vector.tensor_tensor(shift[0:P], neg_mean[0:P], rs[0:P, 0:C], ALU.mult).then_inc(x1_norm, 1)
                if k == K - 1:
                    dve.wait_ge(x1_stored, 16 * (n + 1))
                    dve.wait_ge(h2s_ready, n + 1)
                    assert links[1] == LINKS1, links

            def tail2(n, k):
                links[0] = NB * LINKS1 + n * LINKS2
                if k == 0:
                    links[1] = 0
                    dve.wait_ge(chunk_used, chunks(2, n, K - 1))
                    dve.wait_ge(first_half_saved, NB + n + 1)
                    nc.vector.tensor_tensor(s_t[:], bank_b[:, 0:R], first_half[:], ALU.add).then_inc(s_ready, 1)
                if k == 1:
                    dve.wait_ge(x1_loaded, 16 * (n + 1))
                    link(nc.vector.tensor_tensor(tmp[0:P], x1_in[0:P, 0:C * F].rearrange("p (c f) -> p c f", c=C),
                                                 bl_sb[0:P].unsqueeze(1).to_broadcast([P, C, F]), ALU.add))
                if k == 5:
                    dve.wait_ge(nat_ready, NB + n + 1)
                    for c in range(C):
                        ins = nc.vector.scalar_tensor_tensor(
                            res[0:P, c], nat[0:P, c * F:(c + 1) * F], x1_in[0:P, C * F + c:C * F + c + 1],
                            tmp[0:P, c], ALU.mult, ALU.add)
                    ins.then_inc(res_ready, 1)
                if k == K - 1:
                    dve.wait_ge(out_stored, 16 * (n + 1))
                    assert links[1] == LINKS2, links

            def stream(p, b, first=False):
                for k in range(K):
                    if first and k in SPLITS[p]:
                        split_features(p, k)
                    if k in SPLITS[p]:
                        split_chunk(p, b, k)
                    if p == 1 and k >= 1 and k - 1 in DVE_ACC:
                        sum_chunk(b, k - 1, first)
                    if k == 0 and K - 1 in DVE_ACC:
                        if p == 1 and not first:
                            sum_chunk(b - 1, K - 1)
                        if p == 2 and first:
                            sum_chunk(NB - 1, K - 1)
                    if p == 1 and not first:
                        tail1(b - 1, k)
                    if p == 2 and first:
                        tail1(NB - 1, k)
                    if p == 2 and not first:
                        tail2(b - 1, k)

            dve.wait_ge(consts_loaded, 16 * 6)
            for p in (1, 2):
                stream(p, 0, first=True)
                with dve.Fori(1, NB) as b:
                    stream(p, b)
            for k in range(K):
                tail2(NB - 1, k)

        @block.tensor
        def _(pe):
            def multiply(p, b, k, first):
                bank = (bank_a if k < HALF else bank_b)[:, 0:R]
                opens, closes = k % HALF == 0, k % HALF == HALF - 1
                if k in SPLITS[p]:
                    s = split_slot(p, k)
                    if first:
                        pe.wait_ge(feat_lo_ready, features(p, k))
                    pe.wait_ge(a_hi_ready, splits(p, b, k))
                    for c in range(C):
                        nc.tensor.matmul(bank, feat_hi[0:P, k, c], a_hi[0:P, s, c], start=opens and c == 0, stop=False)
                        nc.tensor.matmul(bank, feat_lo[0:P, k, c], a_hi[0:P, s, c], start=False, stop=False)
                    pe.wait_ge(a_lo_ready, splits(p, b, k))
                    for c in range(C):
                        last = nc.tensor.matmul(bank, feat_hi[0:P, k, c], a_lo[0:P, s, c], start=False,
                                                stop=closes and c == C - 1)
                else:
                    pe.wait_ge(raw_loaded[k % RAW], 16 * loads(p, b, k))
                    for c in range(C):
                        last = nc.tensor.matmul(bank, item_f32[0:P, NATIVE.index(k), c], raw[0:P, k % RAW, c],
                                                start=opens and c == 0, stop=closes and c == C - 1)
                last.then_inc(chunk_used, 1)

            def tail1(n, k):
                if k == 0:
                    pe.wait_ge(summed_dve, sums(DVE_ACC, n, K - 1))
                    pe.wait_ge(summed_pool, sums(POOL_ACC, n, K - 1))
                    for c in range(C):
                        for i, part in enumerate((acc_dve[0:P, 0], acc_dve[0:P, 1], acc_pool[0:P, 0], acc_pool[0:P, 1])):
                            last = nc.tensor.matmul(sums_ps[0:P, c:c + 1], part[:, c * P:(c + 1) * P], ones[0:P],
                                                    start=i == 0, stop=i == 3)
                    last.then_inc(row_sums_ready, 1)
                if k == 5:
                    pe.wait_ge(h0_ready, n + 1)
                    for c in range(C):
                        last = nc.tensor.transpose(h0_ps[:, c * P:(c + 1) * P], h0[0:P, c], ident[0:P, 0:P])
                    last.then_inc(h0_turned, 1)
                if k == 7:
                    pe.wait_ge(s_ready, n + 1)
                    pe.wait_ge(h0_t_ready, n + 1)
                    for c in range(C):
                        nc.tensor.matmul(nat[0:P, c * F:(c + 1) * F], s_t[:, c * P:(c + 1) * P], wi_sb[:],
                                         start=True, stop=False)
                        last = nc.tensor.matmul(nat[0:P, c * F:(c + 1) * F], h0_t[:, c * P:(c + 1) * P], wu_sb[:],
                                                start=False, stop=True)
                    last.then_inc(nat_ready, 1)

            def tail2(n, k):
                if k == 2:
                    pe.wait_ge(s_ready, NB + n + 1)
                    if isinstance(n, int) and n == 0:
                        pe.wait_ge(nat_used, NB)
                    for c in range(C):
                        last = nc.tensor.matmul(nat[0:P, c * F:(c + 1) * F], s_t[:, c * P:(c + 1) * P], w_sb[:],
                                                start=True, stop=True)
                    last.then_inc(nat_ready, 1)

            def stream(p, b, first=False):
                for k in range(K):
                    if k == 0 and not (p == 1 and first):
                        pe.wait_ge(first_half_saved, (p - 1) * NB + b)
                    if k == HALF and not (p == 1 and first):
                        pe.wait_ge(s_ready, (p - 1) * NB + b)
                    multiply(p, b, k, first)
                    if p == 1 and not first:
                        tail1(b - 1, k)
                    if p == 2 and first:
                        tail1(NB - 1, k)
                    if p == 2 and not first:
                        tail2(b - 1, k)

            pe.wait_ge(consts_loaded, 16 * 6)
            pe.wait_ge(native_loaded, 16 * len(NATIVE))
            pe.wait_ge(ident_ready, 2)
            pe.wait_ge(ones_ready, 1)
            for p in (1, 2):
                stream(p, 0, first=True)
                with pe.Fori(1, NB) as b:
                    stream(p, b)
            for k in range(K):
                tail2(NB - 1, k)


def kernel(x, adj, L0_gnn_item_feat, L0_gnn_W_item, L0_gnn_b_item, L0_gnn_W_user, L0_gnn_b_user, L1_gnn_W, L1_gnn_b):
    import numpy as np
    import concourse.bacc as bacc
    from concourse.bass_utils import run_bass_kernel_spmd

    def rows(a):
        return np.ascontiguousarray(np.asarray(a).reshape(NB, C, P, F).transpose(0, 2, 1, 3))

    a = np.asarray(adj).reshape(NB, R, K, C, P)
    blocks = np.zeros((NB, 128, K, C, R), a.dtype)
    for b in range(NB):
        blocks[b, :P] = a[b].transpose(3, 1, 2, 0)
    arrays = {
        "adj": blocks, "items": rows(L0_gnn_item_feat), "xs": rows(x),
        "wi": np.ascontiguousarray(np.asarray(L0_gnn_W_item).T),
        "wu": np.ascontiguousarray(np.asarray(L0_gnn_W_user).T),
        "w": np.ascontiguousarray(np.asarray(L1_gnn_W).T),
        "bi": np.ascontiguousarray(np.broadcast_to(np.asarray(L0_gnn_b_item), (P, F))),
        "bu": np.ascontiguousarray(np.broadcast_to(np.asarray(L0_gnn_b_user), (P, F))),
        "bl": np.ascontiguousarray(np.broadcast_to(np.asarray(L1_gnn_b), (P, F))),
    }
    nc = bacc.Bacc("TRN2", target_bir_lowering=False, num_devices=1)
    ins = [nc.dram_tensor(n, v.shape, mybir.dt.float32, kind="ExternalInput").ap() for n, v in arrays.items()]
    out = nc.dram_tensor("out", (NB, P, C, F), mybir.dt.float32, kind="ExternalOutput").ap()
    gnn_kernel(nc, *ins, out)
    got = run_bass_kernel_spmd(nc, [arrays], core_ids=[0]).results[0]["out"]
    return np.ascontiguousarray(np.asarray(got).reshape(NB, P, C, F).transpose(0, 2, 1, 3)).reshape(N, F)
```

```python
import concourse.bass as bass
from concourse import mybir

N, F = 10000, 128
P = 125
C = 4
R = P * C
NB = N // R
K = N // R
EARLY = 8
RAW, SPLIT, STAGE = 5, 2, 2
EPS = 1e-5
USER_LINKS, TAIL_LINKS = 8, 15
LINKS1, LINKS2 = USER_LINKS + TAIL_LINKS, 2


class Phase:

    def __init__(self, name, p, start, end, order, native, raw, before):
        self.name, self.p, self.start, self.end, self.order = name, p, start, end, order
        self.native, self.raw = native, raw
        self.split = [k not in native for k in order]
        self.chunks0 = before.chunks(before.end, -1) if before else 0
        self.splits0 = before.splits(before.end, -1) if before else 0
        self.loads0 = before.loads(before.end - 1, len(before.order) - 1) if before else 0
        assert len(order) % raw == 0 and sum(self.split) % SPLIT == 0 and raw <= (before.raw if before else RAW)

    def chunks(self, b, pos):
        return self.chunks0 + (b - self.start) * len(self.order) + pos + 1

    def splits(self, b, pos):
        return self.splits0 + (b - self.start) * sum(self.split) + sum(self.split[:pos + 1])

    def loads(self, b, pos):
        return self.loads0 + (b - self.start) * (len(self.order) // self.raw) + pos // self.raw + 1

    def split_slot(self, pos):
        return sum(self.split[:pos]) % SPLIT

    def at(self, k):
        return self.order.index(k)


NATIVE_A = (1, 2, 4, 5, 6, 8, 9, 11, 12, 14, 15, 16, 18, 19)
NATIVE_B = (9, 11, 12, 14, 15, 16, 18, 19)
LATER = list(range(EARLY, K))
A = Phase("A", 1, 0, EARLY, list(range(K)), NATIVE_A, RAW, None)
ORDER_B = [8, 9, 0, 11, 1, 10, 12, 2, 14, 3, 13, 15, 4, 16, 17, 5, 18, 6, 19, 7]
B = Phase("B", 1, EARLY, NB, ORDER_B, NATIVE_B, RAW, A)
CC = Phase("C", 2, 0, EARLY, list(range(K)), (), RAW, B)
D = Phase("D", 2, EARLY, NB, LATER, (), RAW - 1, CC)
PREVIOUS = {"A": None, "B": A, "C": B, "D": CC}


class Job:

    def __init__(self, phase, pos, p, k, after):
        self.pos, self.p, self.k = pos, p, k
        self.slot = feature_slot(p, k)
        self.native = k in phase.native
        self.after = after


PLAIN = [k for k in range(K) if k not in NATIVE_B]
SLOTS = K + EARLY
SPLIT_SLOTS = SLOTS - len(NATIVE_B)
assert set(NATIVE_B) <= set(NATIVE_A) & set(range(EARLY, K)) and len(NATIVE_B) <= EARLY


def feature_slot(p, k):
    if k in NATIVE_B:
        return NATIVE_B.index(k) + (SPLIT_SLOTS if p == 1 else 0)
    return len(PLAIN) + k if p == 2 and k < EARLY else PLAIN.index(k)


def jobs_of(phase):
    jobs = []
    for pos, k in enumerate(phase.order):
        if phase is A:
            jobs.append(Job(A, pos, 1, k, 0))
        if phase is B and k in A.native and k not in B.native:
            jobs.append(Job(B, pos, 1, k, A.chunks(EARLY - 1, A.at(k))))
        if phase is B and k < EARLY:
            jobs.append(Job(B, pos, 2, k, 0))
        if phase is CC and k >= EARLY:
            old = PLAIN[feature_slot(2, k)]
            jobs.append(Job(CC, pos, 2, k, B.chunks(NB - 1, B.at(old))))
    return jobs


JOBS = {"A": jobs_of(A), "B": jobs_of(B), "C": jobs_of(CC), "D": []}
count = 0
for name in "ABC":
    for job in JOBS[name]:
        if not job.native:
            job.number = count
            count += 1


def gnn_kernel(nc, adj, items, xs, wi, wu, w, bi, bu, bl, out):
    f32, f32r = mybir.dt.float32, mybir.dt.float32r
    ALU, ACT = mybir.AluOpType, mybir.ActivationFunctionType

    x1_dram = nc.dram_tensor("x1_and_d", (NB, P, C * F + C), f32, kind="Internal").ap()
    h2_dram = nc.dram_tensor("scaled_h2", (NB, P, C * F), f32, kind="Internal").ap()
    part_dram = nc.dram_tensor("part_of_second", (NB, 128, R), f32, kind="Internal").ap()

    def sb(name, shape, dt=f32):
        return nc.alloc_sbuf_tensor(name, shape, dt)

    low_parts_at = (nc.sbuf_base + 31) // 32 * 32
    feat_lo = sb("feat_lo", [128, SLOTS, C, F], f32r)
    feat_f32 = nc.alloc_sbuf_tensor_at("feat_f32", [128, SLOTS, C, F], f32, offset=low_parts_at)
    feat_hi = sb("feat_hi", [128, SPLIT_SLOTS, C, F], f32r)
    raw = sb("raw", [128, RAW, C, R])
    a_hi = sb("a_hi", [128, SPLIT, C, R], f32r)
    a_lo = sb("a_lo", [128, SPLIT, C, R], f32r)
    stage = sb("stage", [128, STAGE, C, F])
    acc = sb("acc", [128, C, R])
    first_half = sb("first_half", [128, R])
    s_t = sb("s_t", [128, R])
    x_in = sb("x_in", [128, C * F + C])
    h = sb("h", [128, C, F])
    h0_t = sb("h0_t", [128, R])
    part = sb("part", [128, R])
    x1d = sb("x1d", [128, C * F + C])
    tmp = sb("tmp", [128, C, F])
    total = tmp[:].rearrange("p c f -> p (c f)")[:, 0:R]
    res = sb("res", [128, C, F])
    wi_sb, wu_sb, w_sb = sb("wi_sb", [128, F]), sb("wu_sb", [128, F]), sb("w_sb", [128, F])
    bi_sb, bu_sb, bl_sb = sb("bi_sb", [128, F]), sb("bu_sb", [128, F]), sb("bl_sb", [128, F])
    ident = sb("ident", [128, P])
    ones = sb("ones", [128, 1])
    stats = sb("stats", [128, C, 6])
    diff, neg_mean = sb("diff", [128, C]), sb("neg_mean", [128, C])
    sums_sb = sb("sums_sb", [128, C])
    nonzero = sb("nonzero", [128, C])
    val, rec, root = sb("val", [128, 2 * C]), sb("rec", [128, 2 * C]), sb("root", [128, 2 * C])
    newt, rs = sb("newt", [128, 2 * C]), sb("rs", [128, 2 * C])
    shift = sb("shift", [128, C])

    def ps(name):
        return nc.alloc_psum_tensor(name, [128, 512], f32)

    halves = [ps("first_half_ps"), ps("second_half_ps")]
    part_ps = ps("part_ps")
    nat, h0_ps, sums_ps = ps("nat"), ps("h0_ps"), ps("sums_ps")

    def sem(name):
        return nc.alloc_semaphore(name)

    raw_loaded = [sem(f"raw_loaded{i}") for i in range(RAW)]
    stage_loaded = [sem(f"stage_loaded{i}") for i in range(STAGE)]
    native_loaded = {i: sem(f"native_loaded{i}") for i in sorted({j.slot for n in "AB" for j in JOBS[n] if j.native})}
    consts_loaded, x_loaded, x1_loaded, part_loaded = (sem(n) for n in (
        "consts_loaded", "x_loaded", "x1_loaded", "part_loaded"))
    a_hi_ready, a_lo_ready = sem("a_hi_ready"), sem("a_lo_ready")
    a_hi_used, chunk_used = sem("a_hi_used"), sem("chunk_used")
    feat_hi_ready, feat_lo_ready = sem("feat_hi_ready"), sem("feat_lo_ready")
    summed, folded, rows_summed = sem("summed"), sem("folded"), sem("rows_summed")
    first_half_saved, s_ready, part_saved = sem("first_half_saved"), sem("s_ready"), sem("part_saved")
    row_sums_ready, ident_ready, ones_ready = sem("row_sums_ready"), sem("ident_ready"), sem("ones_ready")
    x_rec, x_root, x_norm = sem("x_rec"), sem("x_root"), sem("x_norm")
    h0_ready, h0_turned, h0_t_ready = sem("h0_ready"), sem("h0_turned"), sem("h0_t_ready")
    nat_ready = sem("nat_ready")
    x1_rec, x1_root, x1_norm = sem("x1_rec"), sem("x1_root"), sem("x1_norm")
    h2_ready, h2s_ready, res_ready = sem("h2_ready"), sem("h2s_ready"), sem("res_ready")
    x1_stored, h2_stored, part_stored, out_stored = (sem(n) for n in (
        "x1_stored", "h2_stored", "part_stored", "out_stored"))
    dve_link, nat_read = sem("dve_link"), sem("nat_read")

    def all_blocks(ph, b):
        return (ph.p - 1) * NB + b

    def old_chunk(ph, b, pos):
        if pos >= ph.raw:
            return ph, b, pos - ph.raw
        if isinstance(b, int) and b == ph.start:
            before = PREVIOUS[ph.name]
            return (before, before.end - 1, len(before.order) - before.raw + pos) if before else None
        return ph, b - 1, len(ph.order) - ph.raw + pos

    def tails(ph, b):
        if isinstance(b, int) and b == ph.start:
            before = PREVIOUS[ph.name]
            return (before.p, before.end - 1, before) if before else None
        return ph.p, b - 1, ph

    def run_phases(eng, stream):
        for ph in (A, B, CC, D):
            stream(ph, ph.start, True)
            with eng.Fori(ph.start + 1, ph.end) as b:
                stream(ph, b, False)

    block = nc.Block()
    with block:

        @block.sync
        def _(sp):
            def value(v):
                return v if isinstance(v, int) else sp.to_reg(v)

            def load_chunk(ph, b, pos):
                old = old_chunk(ph, b, pos)
                if old:
                    oph, ob, opos = old
                    if oph.split[opos]:
                        read, count = a_lo_ready, value(oph.splits(ob, opos))
                    else:
                        read, count = chunk_used, value(oph.chunks(ob, opos))
                    if oph.p == 1:
                        sum_count = value(oph.chunks(ob, opos))
                    if ph is B:
                        sp.wait_ge(x_loaded, 16)
                    sp.wait_ge(read, count)
                    if oph.p == 1:
                        sp.wait_ge(summed, sum_count)
                sp.dma_start(raw[:, pos % ph.raw], adj[b, :, ph.order[pos]]).then_inc(raw_loaded[pos % ph.raw], 16)

            def load_features(job):
                src = (items if job.p == 1 else h2_dram)[job.k]
                if job.p == 2:
                    sp.wait_ge(h2_stored, 16 * (job.k + 1))
                if job.native:
                    if job.after:
                        sp.wait_ge(chunk_used, job.after)
                    sp.dma_start(feat_f32[0:P, job.slot], src).then_inc(native_loaded[job.slot], 16)
                else:
                    if job.number >= STAGE:
                        sp.wait_ge(feat_lo_ready, job.number - STAGE + 1)
                    sp.dma_start(stage[0:P, job.number % STAGE], src).then_inc(stage_loaded[job.number % STAGE], 16)

            def store_out(n):
                sp.wait_ge(res_ready, n + 1)
                sp.dma_start(out[n], res[0:P]).then_inc(out_stored, 16)

            def stream(ph, b, first):
                last = len(ph.order) - 1
                for pos in range(-1, last + 1):
                    if pos >= 0:
                        load_chunk(ph, b, pos)
                    if first:
                        for job in JOBS[ph.name]:
                            if job.pos == pos + 1 != last or job.pos == pos == last:
                                load_features(job)
                    if pos == 9 and tails(ph, b) and tails(ph, b)[0] == 2:
                        store_out(tails(ph, b)[1])

            run_phases(sp, stream)
            store_out(NB - 1)
            sp.wait_ge(x1_stored, 16 * NB)
            sp.wait_ge(h2_stored, 16 * NB)
            sp.wait_ge(part_stored, 16 * (NB - EARLY))
            sp.wait_ge(out_stored, 16 * NB)

        @block.gpsimd
        def _(pool):
            nc.gpsimd.memset(ones[:], 1.0).then_inc(ones_ready, 1)
            nc.gpsimd.memset(ident[:], 0.0).then_inc(ident_ready, 1)
            pool.wait_ge(ident_ready, 1)
            nc.gpsimd.affine_select(out=ident[:], in_=ident[:], compare_op=ALU.not_equal, fill=1.0,
                                    base=0, pattern=[[-1, P]], channel_multiplier=1).then_inc(ident_ready, 1)

        @block.scalar
        def _(act):
            act.preload_act_table_set("sqrt_and_others")
            for dst, src in ((wi_sb, wi), (wu_sb, wu), (w_sb, w)):
                act.dma_start(dst[:], src).then_inc(consts_loaded, 16)
            for dst, src in ((bi_sb, bi), (bu_sb, bu), (bl_sb, bl)):
                act.dma_start(dst[0:P], src).then_inc(consts_loaded, 16)

            def split_features(job):
                act.wait_ge(stage_loaded[job.number % STAGE], 16 * (job.number // STAGE + 1))
                if job.after:
                    act.wait_ge(chunk_used, job.after)
                nc.scalar.activation(feat_hi[0:P, job.slot], stage[0:P, job.number % STAGE], ACT.Copy).then_inc(
                    feat_hi_ready, 1)

            def split_chunk(ph, b, pos):
                act.wait_ge(raw_loaded[pos % ph.raw], 16 * ph.loads(b, pos))
                old = ph.splits(b, pos) - SPLIT
                if not (isinstance(old, int) and old <= 0):
                    act.wait_ge(a_hi_used, old)
                    act.wait_ge(a_lo_ready, old)
                nc.scalar.activation(a_hi[0:P, ph.split_slot(pos)], raw[0:P, pos % ph.raw], ACT.Copy).then_inc(
                    a_hi_ready, 1)

            def user_part(n, pos):
                if pos == 10:
                    if not (isinstance(n, int) and n == 0):
                        act.wait_ge(x1_rec, n)
                    act.dma_start(x_in[0:P, 0:C * F], xs[n]).then_inc(x_loaded, 16)
                if pos == 13:
                    act.wait_ge(x_rec, n + 1)
                    nc.scalar.activation(root[0:P, 0:C], rec[0:P, 0:C], ACT.Sqrt).then_inc(x_root, 1)
                if pos == 15:
                    act.wait_ge(x_norm, n + 1)
                    for c in range(C):
                        last = nc.scalar.activation(h[0:P, c], x_in[0:P, c * F:(c + 1) * F], ACT.Relu,
                                                    scale=rs[0:P, c:c + 1], bias=shift[0:P, c:c + 1])
                    last.then_inc(h0_ready, 1)
                if pos == 18:
                    act.wait_ge(h0_turned, n + 1)
                    nc.scalar.activation(h0_t[:], h0_ps[:, 0:R], ACT.Copy).then_inc(h0_t_ready, 1)

            def tail1(n, pos, ph):
                if pos == 1 and ph is B:
                    act.wait_ge(chunk_used, ph.chunks(n, K - 1))
                    nc.scalar.activation(part[:], part_ps[:, 0:R], ACT.Copy).then_inc(part_saved, 1)
                if pos == 2 and ph is B:
                    act.wait_ge(part_saved, n - EARLY + 1)
                    act.dma_start(part_dram[n], part[:]).then_inc(part_stored, 16)
                if pos == 9:
                    act.wait_ge(x1_rec, n + 1)
                    nc.scalar.activation(root[0:P], rec[0:P], ACT.Sqrt).then_inc(x1_root, 1)
                if pos == 11:
                    act.wait_ge(x1_norm, n + 1)
                    for c in range(C):
                        last = nc.scalar.activation(h[0:P, c], x1d[0:P, c * F:(c + 1) * F], ACT.Relu,
                                                    scale=rs[0:P, c:c + 1], bias=shift[0:P, c:c + 1])
                    last.then_inc(h2_ready, 1)
                    act.dma_start(x1_dram[n], x1d[0:P]).then_inc(x1_stored, 16)
                if pos == 12:
                    act.wait_ge(h2_ready, n + 1)
                    for c in range(C):
                        last = nc.scalar.activation(res[0:P, c], h[0:P, c], ACT.Copy,
                                                    scale=x1d[0:P, C * F + c:C * F + c + 1])
                    last.then_inc(h2s_ready, 1)
                if pos == 13:
                    act.wait_ge(h2s_ready, n + 1)
                    act.dma_start(h2_dram[n], res[0:P]).then_inc(h2_stored, 16)
                if pos == K - 1:
                    act.wait_ge(h2_stored, 16 * (n + 1))
                    if ph is B:
                        act.wait_ge(part_stored, 16 * (n - EARLY + 1))

            def load_rows(ph, b, first):
                if ph is CC and first:
                    act.wait_ge(x1_norm, NB)
                    act.wait_ge(x1_stored, 16 * (NB - 1))
                else:
                    act.wait_ge(res_ready, b)
                act.dma_start(x_in[0:P], x1_dram[b]).then_inc(x1_loaded, 16)
                if ph is D:
                    act.wait_ge(part_stored, 16 * (NB - EARLY))
                    act.dma_start(part[:], part_dram[b]).then_inc(part_loaded, 16)

            def stream(ph, b, first):
                half = len(ph.order) // 2
                for pos in range(-1, len(ph.order)):
                    if pos >= 0 and ph.split[pos]:
                        split_chunk(ph, b, pos)
                    if first:
                        for job in JOBS[ph.name]:
                            if job.pos == pos + 1 and not job.native:
                                split_features(job)
                    if pos == half + 1:
                        act.wait_ge(chunk_used, ph.chunks(b, half - 1))
                        if not (ph is A and first):
                            act.wait_ge(s_ready, all_blocks(ph, b))
                        nc.scalar.activation(first_half[:], halves[0][:, 0:R], ACT.Copy).then_inc(first_half_saved, 1)
                    if pos >= 0 and tails(ph, b) and tails(ph, b)[0] == 1:
                        tail1(tails(ph, b)[1], pos, tails(ph, b)[2])
                    if ph.p == 1:
                        user_part(b, pos)
                    elif pos == (9 if ph is D else 16):
                        load_rows(ph, b, first)

            run_phases(act, stream)

        @block.vector
        def _(dve):
            def split_features(job):
                dve.wait_ge(feat_hi_ready, job.number + 1)
                nc.vector.tensor_tensor(feat_lo[0:P, job.slot], stage[0:P, job.number % STAGE],
                                        feat_hi[0:P, job.slot].bitcast(f32), ALU.subtract).then_inc(feat_lo_ready, 1)

            def split_chunk(ph, b, pos):
                s = ph.split_slot(pos)
                dve.wait_ge(a_hi_ready, ph.splits(b, pos))
                before = [i for i in range(pos) if ph.split[i]]
                if len(before) >= SPLIT:
                    dve.wait_ge(chunk_used, ph.chunks(b, before[-SPLIT]))
                elif isinstance(b, int) and b == ph.start:
                    old = PREVIOUS[ph.name]
                    if old:
                        at = [i for i in range(len(old.order)) if old.split[i]][len(before) - SPLIT]
                        dve.wait_ge(chunk_used, old.chunks(old.end - 1, at))
                else:
                    at = [i for i in range(len(ph.order)) if ph.split[i]][len(before) - SPLIT]
                    dve.wait_ge(chunk_used, ph.chunks(b - 1, at))
                nc.vector.tensor_tensor(a_lo[0:P, s], raw[0:P, pos % ph.raw], a_hi[0:P, s].bitcast(f32),
                                        ALU.subtract).then_inc(a_lo_ready, 1)

            def sum_chunk(ph, b, pos):
                if pos == 0:
                    return
                dve.wait_ge(raw_loaded[pos % ph.raw], 16 * ph.loads(b, pos))
                if pos == 1:
                    dve.wait_ge(raw_loaded[0], 16 * ph.loads(b, 0))
                    if not (isinstance(b, int) and b == 0):
                        dve.wait_ge(rows_summed, b)
                    nc.vector.tensor_tensor(acc[0:P], raw[0:P, 0], raw[0:P, 1], ALU.add).then_inc(summed, 2)
                    return
                dve.wait_ge(summed, ph.chunks(b, pos) - 1)
                nc.vector.tensor_tensor(acc[0:P], acc[0:P], raw[0:P, pos % ph.raw], ALU.add).then_inc(summed, 1)
                if pos == K - 1:
                    dve.wait_ge(summed, ph.chunks(b, pos))
                    nc.vector.tensor_tensor(acc[0:P, 0:2], acc[0:P, 0:2], acc[0:P, 2:4], ALU.add).then_inc(folded, 1)
                    dve.wait_ge(folded, b + 1)
                    nc.vector.tensor_tensor(total[0:P], acc[0:P, 0], acc[0:P, 1], ALU.add).then_inc(rows_summed, 1)

            links = [0, 0]

            def link(ins):
                links[1] += 1
                ins.then_inc(dve_link, 1)
                dve.wait_ge(dve_link, links[0] + links[1])

            def norm_stats(src):
                for c in range(C):
                    ins = nc.vector.bn_stats(stats[0:P, c], src[c])
                link(ins)
                even, odd = stats[0:P, :, 0:3], stats[0:P, :, 3:6]
                nc.vector.tensor_tensor(diff[0:P], even[:, :, 1], odd[:, :, 1], ALU.subtract)
                nc.vector.tensor_tensor(neg_mean[0:P], even[:, :, 1], odd[:, :, 1], ALU.add)
                link(nc.vector.tensor_tensor(val[0:P, 0:C], even[:, :, 2], odd[:, :, 2], ALU.add))
                nc.vector.tensor_tensor(diff[0:P], diff[0:P], diff[0:P], ALU.mult)
                nc.vector.tensor_scalar(neg_mean[0:P], neg_mean[0:P], -0.5, None, ALU.mult)
                link(nc.vector.tensor_scalar(val[0:P, 0:C], val[0:P, 0:C], 1.0 / F, EPS, ALU.mult, ALU.add))
                link(nc.vector.scalar_tensor_tensor(val[0:P, 0:C], diff[0:P], 0.25, val[0:P, 0:C], ALU.mult, ALU.add))

            def newton(width):
                link(nc.vector.tensor_tensor(newt[0:P, 0:width], root[0:P, 0:width], root[0:P, 0:width], ALU.mult))
                link(nc.vector.tensor_tensor(newt[0:P, 0:width], newt[0:P, 0:width], val[0:P, 0:width], ALU.mult))
                link(nc.vector.tensor_scalar(newt[0:P, 0:width], newt[0:P, 0:width], -0.5, 1.5, ALU.mult, ALU.add))
                link(nc.vector.tensor_tensor(rs[0:P, 0:width], root[0:P, 0:width], newt[0:P, 0:width], ALU.mult))

            def user_part(n, pos):
                links[0] = n * LINKS1
                if pos == 12:
                    links[1] = 0
                    dve.wait_ge(x_loaded, 16 * (n + 1))
                    norm_stats([x_in[0:P, c * F:(c + 1) * F] for c in range(C)])
                    nc.vector.reciprocal(rec[0:P, 0:C], val[0:P, 0:C]).then_inc(x_rec, 1)
                if pos == 14:
                    dve.wait_ge(x_root, n + 1)
                    if not (isinstance(n, int) and n == 0):
                        dve.wait_ge(h2_ready, n)
                    newton(C)
                    nc.vector.tensor_tensor(shift[0:P], neg_mean[0:P], rs[0:P, 0:C], ALU.mult).then_inc(x_norm, 1)
                    assert links[1] == USER_LINKS, links

            def tail1(n, pos, ph):
                links[0] = USER_LINKS + n * LINKS1
                if pos == 1:
                    links[1] = 0
                    dve.wait_ge(chunk_used, ph.chunks(n, K - 1))
                    dve.wait_ge(first_half_saved, n + 1)
                    nc.vector.tensor_tensor(s_t[:], halves[1][:, 0:R], first_half[:], ALU.add).then_inc(s_ready, 1)
                if pos == 7:
                    dve.wait_ge(row_sums_ready, n + 1)
                    link(nc.vector.tensor_copy(sums_sb[0:P], sums_ps[0:P, 0:C]))
                    dve.wait_ge(nat_ready, n + 1)
                    for c in range(C):
                        ins = nc.vector.scalar_tensor_tensor(tmp[0:P, c], bi_sb[0:P], sums_sb[0:P, c:c + 1],
                                                             nat[0:P, c * F:(c + 1) * F], ALU.mult, ALU.add)
                    ins.then_inc(nat_read, 1)
                    dve.wait_ge(nat_read, n + 1)
                    link(nc.vector.tensor_tensor(tmp[0:P], tmp[0:P], bu_sb[0:P].unsqueeze(1).to_broadcast([P, C, F]),
                                                 ALU.add))
                    link(nc.vector.scalar_tensor_tensor(
                        x1d[0:P, 0:C * F], tmp[0:P].rearrange("p c f -> p (c f)"), 0.0,
                        x_in[0:P, 0:C * F], ALU.max, ALU.add))
                if pos == 8:
                    dve.wait_ge(h0_ready, n + 1)
                    norm_stats([x1d[0:P, c * F:(c + 1) * F] for c in range(C)])
                    link(nc.vector.tensor_scalar(nonzero[0:P], sums_sb[0:P], 0.0, None, ALU.is_equal))
                    link(nc.vector.tensor_tensor(val[0:P, C:2 * C], sums_sb[0:P], nonzero[0:P], ALU.add))
                    nc.vector.reciprocal(rec[0:P], val[0:P]).then_inc(x1_rec, 1)
                    link(nc.vector.tensor_scalar(nonzero[0:P], nonzero[0:P], -1.0, 1.0, ALU.mult, ALU.add))
                if pos == 10:
                    dve.wait_ge(x1_root, n + 1)
                    newton(2 * C)
                    link(nc.vector.tensor_tensor(x1d[0:P, C * F:], rs[0:P, C:2 * C], nonzero[0:P], ALU.mult))
                    nc.vector.tensor_tensor(shift[0:P], neg_mean[0:P], rs[0:P, 0:C], ALU.mult).then_inc(x1_norm, 1)
                    assert links[1] == TAIL_LINKS, links
                if pos == K - 1:
                    dve.wait_ge(x1_stored, 16 * (n + 1))
                    dve.wait_ge(h2s_ready, n + 1)

            def tail2(n, pos, ph, last):
                links[0] = NB * LINKS1 + (n if ph is CC else EARLY + (n - EARLY) * LINKS2)
                if pos == 1:
                    links[1] = 0
                    dve.wait_ge(chunk_used, ph.chunks(n, len(ph.order) - 1))
                    dve.wait_ge(first_half_saved, NB + n + 1)
                    ins = nc.vector.tensor_tensor(s_t[:], halves[1][:, 0:R], first_half[:], ALU.add)
                    if ph is D:
                        link(ins)
                        dve.wait_ge(part_loaded, 16 * (n - EARLY + 1))
                        ins = nc.vector.tensor_tensor(s_t[:], s_t[:], part[:], ALU.add)
                    ins.then_inc(s_ready, 1)
                if pos == 2:
                    dve.wait_ge(x1_loaded, 16 * (n + 1))
                    link(nc.vector.tensor_tensor(tmp[0:P], x_in[0:P, 0:C * F].rearrange("p (c f) -> p c f", c=C),
                                                 bl_sb[0:P].unsqueeze(1).to_broadcast([P, C, F]), ALU.add))
                if pos == 6:
                    dve.wait_ge(nat_ready, NB + n + 1)
                    for c in range(C):
                        ins = nc.vector.scalar_tensor_tensor(
                            res[0:P, c], nat[0:P, c * F:(c + 1) * F], x_in[0:P, C * F + c:C * F + c + 1],
                            tmp[0:P, c], ALU.mult, ALU.add)
                    ins.then_inc(res_ready, 1)
                if pos == last:
                    dve.wait_ge(out_stored, 16 * (n + 1))
                    assert links[1] == (1 if ph is CC else LINKS2), links

            def stream(ph, b, first):
                last = len(ph.order) - 1
                for pos in range(-1, last + 1):
                    if pos >= 0 and ph.split[pos]:
                        split_chunk(ph, b, pos)
                    if first:
                        for job in JOBS[ph.name]:
                            if job.pos == pos + 1 and not job.native:
                                split_features(job)
                    if ph.p == 1 and pos >= 0:
                        sum_chunk(ph, b, pos)
                    if pos >= 0 and tails(ph, b):
                        p, n, before = tails(ph, b)
                        if p == 1:
                            tail1(n, pos, before)
                        else:
                            tail2(n, pos, before, last)
                    if ph.p == 1:
                        user_part(b, pos)

            dve.wait_ge(consts_loaded, 16 * 6)
            run_phases(dve, stream)
            for pos in range(K):
                tail2(NB - 1, pos, D, K - 1)

        @block.tensor
        def _(pe):
            def multiply(ph, b, pos, first):
                k, half = ph.order[pos], len(ph.order) // 2
                within = pos % half
                made = [(halves[pos // half][:, 0:R], feature_slot(ph.p, k), within == 0, within == half - 1)]
                if ph is B and k < EARLY:
                    made.append((part_ps[:, 0:R], feature_slot(2, k), k == 0, k == EARLY - 1))
                if first:
                    jobs = [j for j in JOBS[ph.name] if j.pos == pos]
                    for j in jobs:
                        if j.native:
                            pe.wait_ge(native_loaded[j.slot], 16)
                        elif j is jobs[-1] or jobs[-1].native:
                            pe.wait_ge(feat_lo_ready, j.number + 1)
                buf = raw[0:P, pos % ph.raw]
                if not ph.split[pos]:
                    pe.wait_ge(raw_loaded[pos % ph.raw], 16 * ph.loads(b, pos))
                    for bank, slot, opens, closes in made:
                        for t in range(C):
                            last = nc.tensor.matmul(bank, feat_f32[0:P, slot, t], buf[:, t],
                                                    start=opens and t == 0, stop=closes and t == C - 1)
                    last.then_inc(chunk_used, 1)
                    return
                s = ph.split_slot(pos)
                pe.wait_ge(a_hi_ready, ph.splits(b, pos))
                for bank, slot, opens, closes in made:
                    for t in range(C):
                        nc.tensor.matmul(bank, feat_lo[0:P, slot, t], a_hi[0:P, s, t], start=opens and t == 0,
                                         stop=False)
                        last = nc.tensor.matmul(bank, feat_hi[0:P, slot, t], a_hi[0:P, s, t], start=False, stop=False)
                last.then_inc(a_hi_used, 1)
                pe.wait_ge(a_lo_ready, ph.splits(b, pos))
                for bank, slot, opens, closes in made:
                    for t in range(C):
                        last = nc.tensor.matmul(bank, feat_hi[0:P, slot, t], a_lo[0:P, s, t], start=False,
                                                stop=closes and t == C - 1)
                last.then_inc(chunk_used, 1)

            def row_sums(n):
                pe.wait_ge(rows_summed, n + 1)
                for c in range(C):
                    last = nc.tensor.matmul(sums_ps[0:P, c:c + 1], total[0:P, c * P:(c + 1) * P], ones[0:P],
                                            start=True, stop=True)
                last.then_inc(row_sums_ready, 1)

            def tail1(n, pos):
                if pos == 1:
                    row_sums(n)
                if pos == 4:
                    pe.wait_ge(s_ready, n + 1)
                    pe.wait_ge(h0_t_ready, n + 1)
                    for c in range(C):
                        nc.tensor.matmul(nat[0:P, c * F:(c + 1) * F], s_t[:, c * P:(c + 1) * P], wi_sb[:],
                                         start=True, stop=False)
                        last = nc.tensor.matmul(nat[0:P, c * F:(c + 1) * F], h0_t[:, c * P:(c + 1) * P], wu_sb[:],
                                                start=False, stop=True)
                    last.then_inc(nat_ready, 1)

            def user_part(n, pos):
                if pos == 16:
                    pe.wait_ge(h0_ready, n + 1)
                    for c in range(C):
                        last = nc.tensor.transpose(h0_ps[:, c * P:(c + 1) * P], h[0:P, c], ident[0:P, 0:P])
                    last.then_inc(h0_turned, 1)

            def tail2(n, pos):
                if pos == 3:
                    pe.wait_ge(s_ready, NB + n + 1)
                    for c in range(C):
                        last = nc.tensor.matmul(nat[0:P, c * F:(c + 1) * F], s_t[:, c * P:(c + 1) * P], w_sb[:],
                                                start=True, stop=True)
                    last.then_inc(nat_ready, 1)

            def stream(ph, b, first):
                half = len(ph.order) // 2
                for pos in range(len(ph.order)):
                    if pos == 0 and tails(ph, b):
                        pe.wait_ge(first_half_saved, all_blocks(ph, b))
                    if pos == half and tails(ph, b):
                        pe.wait_ge(s_ready, all_blocks(ph, b))
                    if ph is B and not first and ph.order[pos] == 0:
                        pe.wait_ge(part_saved, b - EARLY)
                    multiply(ph, b, pos, first)
                    if tails(ph, b):
                        p, n, before = tails(ph, b)
                        if p == 1:
                            tail1(n, pos)
                        else:
                            tail2(n, pos)
                    if ph.p == 1:
                        user_part(b, pos)

            pe.wait_ge(consts_loaded, 16 * 6)
            pe.wait_ge(ident_ready, 2)
            pe.wait_ge(ones_ready, 1)
            run_phases(pe, stream)
            for pos in range(K):
                tail2(NB - 1, pos)


def kernel(x, adj, L0_gnn_item_feat, L0_gnn_W_item, L0_gnn_b_item, L0_gnn_W_user, L0_gnn_b_user, L1_gnn_W, L1_gnn_b):
    import numpy as np
    import concourse.bacc as bacc
    from concourse.bass_utils import run_bass_kernel_spmd

    def rows(a):
        return np.ascontiguousarray(np.asarray(a).reshape(NB, C, P, F).transpose(0, 2, 1, 3))

    a = np.asarray(adj).reshape(NB, R, K, C, P)
    blocks = np.zeros((NB, 128, K, C, R), a.dtype)
    for b in range(NB):
        blocks[b, :P] = a[b].transpose(3, 1, 2, 0)
    arrays = {
        "adj": blocks, "items": rows(L0_gnn_item_feat), "xs": rows(x),
        "wi": np.ascontiguousarray(np.asarray(L0_gnn_W_item).T),
        "wu": np.ascontiguousarray(np.asarray(L0_gnn_W_user).T),
        "w": np.ascontiguousarray(np.asarray(L1_gnn_W).T),
        "bi": np.ascontiguousarray(np.broadcast_to(np.asarray(L0_gnn_b_item), (P, F))),
        "bu": np.ascontiguousarray(np.broadcast_to(np.asarray(L0_gnn_b_user), (P, F))),
        "bl": np.ascontiguousarray(np.broadcast_to(np.asarray(L1_gnn_b), (P, F))),
    }
    nc = bacc.Bacc("TRN2", target_bir_lowering=False, num_devices=1)
    ins = [nc.dram_tensor(n, v.shape, mybir.dt.float32, kind="ExternalInput").ap() for n, v in arrays.items()]
    out = nc.dram_tensor("out", (NB, P, C, F), mybir.dt.float32, kind="ExternalOutput").ap()
    gnn_kernel(nc, *ins, out)
    got = run_bass_kernel_spmd(nc, [arrays], core_ids=[0]).results[0]["out"]
    return np.ascontiguousarray(np.asarray(got).reshape(NB, P, C, F).transpose(0, 2, 1, 3)).reshape(N, F)
```

```python
import concourse.bass as bass
from concourse import mybir

N, F = 10000, 128
P = 125
C = 4
R = P * C
NB = N // R
K = N // R
EARLY = 8
RAW, SPLIT, STAGE = 5, 2, 4
EPS = 1e-5
FIRST_LINKS, LINKS1, LINKS2 = 8, 12, 2


class Phase:

    def __init__(self, name, p, start, end, order, native, raw, before):
        self.name, self.p, self.start, self.end, self.order = name, p, start, end, order
        self.native, self.raw = native, raw
        self.split = [k not in native for k in order]
        self.chunks0 = before.chunks(before.end, -1) if before else 0
        self.splits0 = before.splits(before.end, -1) if before else 0
        self.loads0 = before.loads(before.end - 1, len(before.order) - 1) if before else 0
        assert len(order) % raw == 0 and sum(self.split) % SPLIT == 0 and raw <= (before.raw if before else RAW)

    def chunks(self, b, pos):
        return self.chunks0 + (b - self.start) * len(self.order) + pos + 1

    def splits(self, b, pos):
        return self.splits0 + (b - self.start) * sum(self.split) + sum(self.split[:pos + 1])

    def loads(self, b, pos):
        return self.loads0 + (b - self.start) * (len(self.order) // self.raw) + pos // self.raw + 1

    def split_slot(self, pos):
        return sum(self.split[:pos]) % SPLIT

    def at(self, k):
        return self.order.index(k)


NATIVE_A = (1, 2, 4, 5, 6, 8, 9, 11, 12, 14, 15, 16, 18, 19)
NATIVE_B = (9, 11, 12, 14, 15, 16, 18, 19)
LATER = list(range(EARLY, K))
A = Phase("A", 1, 0, EARLY, list(range(K)), NATIVE_A, RAW, None)
ORDER_B = [8, 9, 0, 11, 1, 10, 12, 2, 14, 3, 13, 15, 4, 16, 17, 5, 18, 6, 19, 7]
B = Phase("B", 1, EARLY, NB, ORDER_B, NATIVE_B, RAW, A)
CC = Phase("C", 2, 0, EARLY, list(range(K)), (), RAW, B)
D = Phase("D", 2, EARLY, NB, LATER, (), RAW - 1, CC)
PREVIOUS = {"A": None, "B": A, "C": B, "D": CC}


class Job:

    def __init__(self, phase, pos, p, k, after):
        self.pos, self.p, self.k = pos, p, k
        self.slot = feature_slot(p, k)
        self.native = k in phase.native
        self.after = after


PLAIN = [k for k in range(K) if k not in NATIVE_B]
SLOTS = K + EARLY
SPLIT_SLOTS = SLOTS - len(NATIVE_B)
assert set(NATIVE_B) <= set(NATIVE_A) & set(range(EARLY, K)) and len(NATIVE_B) <= EARLY


def feature_slot(p, k):
    if k in NATIVE_B:
        return NATIVE_B.index(k) + (SPLIT_SLOTS if p == 1 else 0)
    return len(PLAIN) + k if p == 2 and k < EARLY else PLAIN.index(k)


def jobs_of(phase):
    jobs = []
    for pos, k in enumerate(phase.order):
        if phase is A:
            jobs.append(Job(A, pos, 1, k, 0))
        if phase is B and k in A.native and k not in B.native:
            jobs.append(Job(B, pos, 1, k, A.chunks(EARLY - 1, A.at(k))))
        if phase is B and k < EARLY:
            jobs.append(Job(B, pos, 2, k, 0))
        if phase is CC and k >= EARLY:
            old = PLAIN[feature_slot(2, k)]
            jobs.append(Job(CC, pos, 2, k, B.chunks(NB - 1, B.at(old))))
    return jobs


JOBS = {"A": jobs_of(A), "B": jobs_of(B), "C": jobs_of(CC), "D": []}
count = 0
for name in "ABC":
    for job in JOBS[name]:
        if not job.native:
            job.number = count
            count += 1


def gnn_kernel(nc, adj, items, xs, wi, wu, w, bi, bu, bl, out):
    f32, f32r = mybir.dt.float32, mybir.dt.float32r
    ALU, ACT = mybir.AluOpType, mybir.ActivationFunctionType

    x1_dram = nc.dram_tensor("x1_and_d", (NB, 128, C * F + C), f32, kind="Internal").ap()
    h2_dram = nc.dram_tensor("scaled_h2", (NB, 128, C * F), f32, kind="Internal").ap()
    part_dram = nc.dram_tensor("part_of_second", (NB, 128, R), f32, kind="Internal").ap()

    def sb(name, shape, dt=f32):
        return nc.alloc_sbuf_tensor(name, shape, dt)

    low_parts_at = (nc.sbuf_base + 31) // 32 * 32
    feat_lo = sb("feat_lo", [128, SLOTS, C, F], f32r)
    feat_f32 = nc.alloc_sbuf_tensor_at("feat_f32", [128, SLOTS, C, F], f32, offset=low_parts_at)
    feat_hi = sb("feat_hi", [128, SPLIT_SLOTS, C, F], f32r)
    raw = sb("raw", [128, RAW, C, R])
    a_hi = sb("a_hi", [128, SPLIT, C, R], f32r)
    a_lo = sb("a_lo", [128, SPLIT, C, R], f32r)
    stage = sb("stage", [128, STAGE, C, F])
    acc = sb("acc", [128, C, R])
    first_half = sb("first_half", [128, R])
    s_t = sb("s_t", [128, R])
    x_in = sb("x_in", [128, C * F + C])
    h0, h2 = sb("h0", [128, C, F]), sb("h2", [128, C, F])
    h0_t = sb("h0_t", [128, R])
    part = sb("part", [128, R])
    x1d = sb("x1d", [128, C * F + C])
    tmp = sb("tmp", [128, C, F])
    total = tmp[:].rearrange("p c f -> p (c f)")[:, 0:R]
    res = sb("res", [128, C, F])
    wi_sb, wu_sb, w_sb = sb("wi_sb", [128, F]), sb("wu_sb", [128, F]), sb("w_sb", [128, F])
    bi_sb, bu_sb, bl_sb = sb("bi_sb", [128, F]), sb("bu_sb", [128, F]), sb("bl_sb", [128, F])
    ident = sb("ident", [128, P])
    ones = sb("ones", [128, 1])
    stats = sb("stats", [128, 2 * C, 6])
    diff, neg_mean = sb("diff", [128, 2 * C]), sb("neg_mean", [128, 2 * C])
    val, rec, root = sb("val", [128, 3 * C]), sb("rec", [128, 3 * C]), sb("root", [128, 3 * C])
    newt, rs = sb("newt", [128, 3 * C]), sb("rs", [128, 3 * C])
    shift = sb("shift", [128, 2 * C])
    sums_sb = sb("sums_sb", [128, C])
    nonzero = sb("nonzero", [128, C])

    def ps(name):
        return nc.alloc_psum_tensor(name, [128, 512], f32)

    halves = [ps("first_half_ps"), ps("second_half_ps")]
    part_ps = ps("part_ps")
    nat, h0_ps, sums_ps = ps("nat"), ps("h0_ps"), ps("sums_ps")

    def sem(name):
        return nc.alloc_semaphore(name)

    raw_loaded = [sem(f"raw_loaded{i}") for i in range(RAW)]
    stage_loaded = [sem(f"stage_loaded{i}") for i in range(STAGE)]
    native_loaded = {i: sem(f"native_loaded{i}") for i in sorted({j.slot for n in "AB" for j in JOBS[n] if j.native})}
    consts_loaded, x_loaded, x1_loaded, part_loaded = (sem(n) for n in (
        "consts_loaded", "x_loaded", "x1_loaded", "part_loaded"))
    a_hi_ready, a_lo_ready = sem("a_hi_ready"), sem("a_lo_ready")
    a_hi_used, chunk_used = sem("a_hi_used"), sem("chunk_used")
    feat_hi_ready, feat_lo_ready = sem("feat_hi_ready"), sem("feat_lo_ready")
    summed, folded, rows_summed = sem("summed"), sem("folded"), sem("rows_summed")
    first_half_saved, s_ready, part_saved = sem("first_half_saved"), sem("s_ready"), sem("part_saved")
    row_sums_ready, ident_ready, ones_ready = sem("row_sums_ready"), sem("ident_ready"), sem("ones_ready")
    norm_rec, norm_root, norm_ready = sem("norm_rec"), sem("norm_root"), sem("norm_ready")
    h0_ready, h0_turned, h0_t_ready = sem("h0_ready"), sem("h0_turned"), sem("h0_t_ready")
    nat_ready, x_used = sem("nat_ready"), sem("x_used")
    h2_ready, h2s_ready, res_ready = sem("h2_ready"), sem("h2s_ready"), sem("res_ready")
    x1_stored, h2_stored, part_stored, out_stored = (sem(n) for n in (
        "x1_stored", "h2_stored", "part_stored", "out_stored"))
    dve_link, nat_read, cleared = sem("dve_link"), sem("nat_read"), sem("cleared")

    def all_blocks(ph, b):
        return (ph.p - 1) * NB + b

    def old_chunk(ph, b, pos):
        if pos >= ph.raw:
            return ph, b, pos - ph.raw
        if isinstance(b, int) and b == ph.start:
            before = PREVIOUS[ph.name]
            return (before, before.end - 1, len(before.order) - before.raw + pos) if before else None
        return ph, b - 1, len(ph.order) - ph.raw + pos

    def tails(ph, b):
        if isinstance(b, int) and b == ph.start:
            before = PREVIOUS[ph.name]
            return (before.p, before.end - 1, before) if before else None
        return ph.p, b - 1, ph

    def run_phases(eng, stream):
        for ph in (A, B, CC, D):
            stream(ph, ph.start, True)
            with eng.Fori(ph.start + 1, ph.end) as b:
                stream(ph, b, False)

    block = nc.Block()
    with block:

        @block.sync
        def _(sp):
            def value(v):
                return v if isinstance(v, int) else sp.to_reg(v)

            def load_chunk(ph, b, pos):
                old = old_chunk(ph, b, pos)
                if old:
                    oph, ob, opos = old
                    if oph.split[opos]:
                        read, count = a_lo_ready, value(oph.splits(ob, opos))
                    else:
                        read, count = chunk_used, value(oph.chunks(ob, opos))
                    if oph.p == 1:
                        sum_count = value(oph.chunks(ob, opos))
                    if ph is B:
                        sp.wait_ge(x_loaded, 16)
                    sp.wait_ge(read, count)
                    if oph.p == 1:
                        sp.wait_ge(summed, sum_count)
                sp.dma_start(raw[:, pos % ph.raw], adj[b, ph.order[pos]]).then_inc(raw_loaded[pos % ph.raw], 16)

            def load_features(job):
                src = (items if job.p == 1 else h2_dram)[job.k]
                if job.p == 2:
                    sp.wait_ge(h2_stored, 16 * (job.k + 1))
                if job.native:
                    if job.after:
                        sp.wait_ge(chunk_used, job.after)
                    sp.dma_start(feat_f32[:, job.slot], src).then_inc(native_loaded[job.slot], 16)
                else:
                    if job.number >= STAGE:
                        sp.wait_ge(feat_lo_ready, job.number - STAGE + 1)
                    sp.dma_start(stage[:, job.number % STAGE], src).then_inc(stage_loaded[job.number % STAGE], 16)

            def store_out(n):
                sp.wait_ge(res_ready, n + 1)
                sp.dma_start(out[n], res[:]).then_inc(out_stored, 16)

            def stream(ph, b, first):
                last = len(ph.order) - 1
                for pos in range(-1, last + 1):
                    if pos >= 0:
                        load_chunk(ph, b, pos)
                    if first:
                        for job in JOBS[ph.name]:
                            if job.pos == pos + 1 != last or job.pos == pos == last:
                                load_features(job)
                    if pos == 9 and tails(ph, b) and tails(ph, b)[0] == 2:
                        store_out(tails(ph, b)[1])

            run_phases(sp, stream)
            store_out(NB - 1)
            sp.wait_ge(x1_stored, 16 * NB)
            sp.wait_ge(h2_stored, 16 * NB)
            sp.wait_ge(part_stored, 16 * (NB - EARLY))
            sp.wait_ge(out_stored, 16 * NB)

        @block.gpsimd
        def _(pool):
            nc.gpsimd.memset(ones[:], 1.0).then_inc(ones_ready, 1)
            nc.gpsimd.memset(ident[:], 0.0).then_inc(ident_ready, 1)
            pool.wait_ge(ident_ready, 1)
            nc.gpsimd.affine_select(out=ident[:], in_=ident[:], compare_op=ALU.not_equal, fill=1.0,
                                    base=0, pattern=[[-1, P]], channel_multiplier=1).then_inc(ident_ready, 1)

        @block.scalar
        def _(act):
            act.preload_act_table_set("sqrt_and_others")

            def split_features(job):
                act.wait_ge(stage_loaded[job.number % STAGE], 16 * (job.number // STAGE + 1))
                if job.after:
                    act.wait_ge(chunk_used, job.after)
                nc.scalar.activation(feat_hi[0:P, job.slot], stage[0:P, job.number % STAGE], ACT.Copy).then_inc(
                    feat_hi_ready, 1)

            def split_chunk(ph, b, pos):
                act.wait_ge(raw_loaded[pos % ph.raw], 16 * ph.loads(b, pos))
                old = ph.splits(b, pos) - SPLIT
                if not (isinstance(old, int) and old <= 0):
                    act.wait_ge(a_hi_used, old)
                    act.wait_ge(a_lo_ready, old)
                nc.scalar.activation(a_hi[0:P, ph.split_slot(pos)], raw[0:P, pos % ph.raw], ACT.Copy).then_inc(
                    a_hi_ready, 1)

            def load_constants():
                for dst, src in ((wi_sb, wi), (wu_sb, wu), (w_sb, w), (bi_sb, bi), (bu_sb, bu), (bl_sb, bl)):
                    act.dma_start(dst[:], src).then_inc(consts_loaded, 16)

            def norms(b, pos, user, tail):
                low, high = (0 if user else C), (3 * C if tail else C)
                if pos == 8 and user:
                    if tail:
                        act.wait_ge(x_used, b)
                    act.dma_start(x_in[:, 0:C * F], xs[b]).then_inc(x_loaded, 16)
                if pos == 11:
                    act.wait_ge(norm_rec, b + 1)
                    nc.scalar.activation(root[0:P, low:high], rec[0:P, low:high], ACT.Sqrt).then_inc(norm_root, 1)
                if pos == 13:
                    act.wait_ge(norm_ready, b + 1)
                    if tail:
                        for c in range(C):
                            last = nc.scalar.activation(h2[0:P, c], x1d[0:P, c * F:(c + 1) * F], ACT.Relu,
                                                        scale=rs[0:P, C + c:C + c + 1],
                                                        bias=shift[0:P, C + c:C + c + 1])
                        last.then_inc(h2_ready, 1)
                        act.dma_start(x1_dram[b - 1], x1d[:]).then_inc(x1_stored, 16)
                    if user:
                        for c in range(C):
                            last = nc.scalar.activation(h0[0:P, c], x_in[0:P, c * F:(c + 1) * F], ACT.Relu,
                                                        scale=rs[0:P, c:c + 1], bias=shift[0:P, c:c + 1])
                        last.then_inc(h0_ready, 1)
                if pos == 18 and user:
                    act.wait_ge(h0_turned, b + 1)
                    nc.scalar.activation(h0_t[:], h0_ps[:, 0:R], ACT.Copy).then_inc(h0_t_ready, 1)

            def tail1(n, pos, ph):
                if pos == 1 and ph is B:
                    act.wait_ge(chunk_used, ph.chunks(n, K - 1))
                    nc.scalar.activation(part[:], part_ps[:, 0:R], ACT.Copy).then_inc(part_saved, 1)
                if pos == 2 and ph is B:
                    act.wait_ge(part_saved, n - EARLY + 1)
                    act.dma_start(part_dram[n], part[:]).then_inc(part_stored, 16)
                if pos == 14:
                    act.wait_ge(h2_ready, n + 1)
                    for c in range(C):
                        last = nc.scalar.activation(res[0:P, c], h2[0:P, c], ACT.Copy,
                                                    scale=x1d[0:P, C * F + c:C * F + c + 1])
                    last.then_inc(h2s_ready, 1)
                if pos == 15:
                    act.wait_ge(h2s_ready, n + 1)
                    act.dma_start(h2_dram[n], res[:]).then_inc(h2_stored, 16)
                if pos == K - 1:
                    act.wait_ge(h2_stored, 16 * (n + 1))
                    if ph is B:
                        act.wait_ge(part_stored, 16 * (n - EARLY + 1))

            def load_rows(ph, b, first):
                if ph is CC and first:
                    act.wait_ge(x_used, NB)
                    act.wait_ge(x1_stored, 16 * (NB - 1))
                else:
                    act.wait_ge(res_ready, b)
                act.dma_start(x_in[:], x1_dram[b]).then_inc(x1_loaded, 16)
                if ph is D:
                    act.wait_ge(part_stored, 16 * (NB - EARLY))
                    act.dma_start(part[:], part_dram[b]).then_inc(part_loaded, 16)

            def stream(ph, b, first):
                half = len(ph.order) // 2
                for pos in range(-1, len(ph.order)):
                    if pos >= 0 and ph.split[pos]:
                        split_chunk(ph, b, pos)
                    if first:
                        for job in JOBS[ph.name]:
                            if job.pos == pos + 1 and not job.native:
                                split_features(job)
                    if pos == half + 1:
                        act.wait_ge(chunk_used, ph.chunks(b, half - 1))
                        if not (ph is A and first):
                            act.wait_ge(s_ready, all_blocks(ph, b))
                        nc.scalar.activation(first_half[:], halves[0][:, 0:R], ACT.Copy).then_inc(first_half_saved, 1)
                    if pos >= 0 and tails(ph, b) and tails(ph, b)[0] == 1:
                        tail1(tails(ph, b)[1], pos, tails(ph, b)[2])
                    if ph.p == 1 or ph is CC and first:
                        norms(all_blocks(ph, b), pos, ph.p == 1, bool(tails(ph, b)))
                    if ph is A and first and pos == 3:
                        load_constants()
                    if ph.p == 2 and pos == (9 if ph is D else 16):
                        load_rows(ph, b, first)

            run_phases(act, stream)

        @block.vector
        def _(dve):
            def split_features(job):
                dve.wait_ge(feat_hi_ready, job.number + 1)
                nc.vector.tensor_tensor(feat_lo[0:P, job.slot], stage[0:P, job.number % STAGE],
                                        feat_hi[0:P, job.slot].bitcast(f32), ALU.subtract).then_inc(feat_lo_ready, 1)

            def split_chunk(ph, b, pos):
                s = ph.split_slot(pos)
                dve.wait_ge(a_hi_ready, ph.splits(b, pos))
                before = [i for i in range(pos) if ph.split[i]]
                if len(before) >= SPLIT:
                    dve.wait_ge(chunk_used, ph.chunks(b, before[-SPLIT]))
                elif isinstance(b, int) and b == ph.start:
                    old = PREVIOUS[ph.name]
                    if old:
                        at = [i for i in range(len(old.order)) if old.split[i]][len(before) - SPLIT]
                        dve.wait_ge(chunk_used, old.chunks(old.end - 1, at))
                else:
                    at = [i for i in range(len(ph.order)) if ph.split[i]][len(before) - SPLIT]
                    dve.wait_ge(chunk_used, ph.chunks(b - 1, at))
                nc.vector.tensor_tensor(a_lo[0:P, s], raw[0:P, pos % ph.raw], a_hi[0:P, s].bitcast(f32),
                                        ALU.subtract).then_inc(a_lo_ready, 1)

            def sum_chunk(ph, b, pos):
                if pos == 0:
                    return
                dve.wait_ge(raw_loaded[pos % ph.raw], 16 * ph.loads(b, pos))
                if pos == 1:
                    dve.wait_ge(raw_loaded[0], 16 * ph.loads(b, 0))
                    if not (isinstance(b, int) and b == 0):
                        dve.wait_ge(rows_summed, b)
                    nc.vector.tensor_tensor(acc[0:P], raw[0:P, 0], raw[0:P, 1], ALU.add).then_inc(summed, 2)
                    return
                dve.wait_ge(summed, ph.chunks(b, pos) - 1)
                nc.vector.tensor_tensor(acc[0:P], acc[0:P], raw[0:P, pos % ph.raw], ALU.add).then_inc(summed, 1)
                if pos == K - 1:
                    dve.wait_ge(summed, ph.chunks(b, pos))
                    nc.vector.tensor_tensor(acc[0:P, 0:2], acc[0:P, 0:2], acc[0:P, 2:4], ALU.add).then_inc(folded, 1)
                    dve.wait_ge(folded, b + 1)
                    nc.vector.tensor_tensor(total[0:P], acc[0:P, 0], acc[0:P, 1], ALU.add).then_inc(rows_summed, 1)

            links = [0, 0]

            def link(ins):
                links[1] += 1
                ins.then_inc(dve_link, 1)
                dve.wait_ge(dve_link, links[0] + links[1])

            def norms(b, pos, user, tail):
                low, mid, high = (0 if user else C), (2 * C if tail else C), (3 * C if tail else C)
                s_, v_ = (slice(0, P), slice(low, mid)), (slice(0, P), slice(low, high))
                if pos == 10:
                    if user:
                        dve.wait_ge(x_loaded, 16 * (b + 1))
                        for c in range(C):
                            ins = nc.vector.bn_stats(stats[0:P, c], x_in[0:P, c * F:(c + 1) * F])
                    if tail:
                        dve.wait_ge(x_used, b)
                        for c in range(C):
                            ins = nc.vector.bn_stats(stats[0:P, C + c], x1d[0:P, c * F:(c + 1) * F])
                    link(ins)
                    even, odd = stats[0:P, low:mid, 0:3], stats[0:P, low:mid, 3:6]
                    nc.vector.tensor_tensor(diff[s_], even[:, :, 1], odd[:, :, 1], ALU.subtract)
                    nc.vector.tensor_tensor(neg_mean[s_], even[:, :, 1], odd[:, :, 1], ALU.add)
                    link(nc.vector.tensor_tensor(val[s_], even[:, :, 2], odd[:, :, 2], ALU.add))
                    nc.vector.tensor_tensor(diff[s_], diff[s_], diff[s_], ALU.mult)
                    nc.vector.tensor_scalar(neg_mean[s_], neg_mean[s_], -0.5, None, ALU.mult)
                    if tail:
                        nc.vector.tensor_scalar(nonzero[0:P], sums_sb[0:P], 0.0, None, ALU.is_equal)
                    link(nc.vector.tensor_scalar(val[s_], val[s_], 1.0 / F, EPS, ALU.mult, ALU.add))
                    if tail:
                        nc.vector.tensor_tensor(val[0:P, 2 * C:], sums_sb[0:P], nonzero[0:P], ALU.add)
                    link(nc.vector.scalar_tensor_tensor(val[s_], diff[s_], 0.25, val[s_], ALU.mult, ALU.add))
                    nc.vector.reciprocal(rec[v_], val[v_]).then_inc(norm_rec, 1)
                    if tail:
                        link(nc.vector.tensor_scalar(nonzero[0:P], nonzero[0:P], -1.0, 1.0, ALU.mult, ALU.add))
                if pos == 12:
                    dve.wait_ge(norm_root, b + 1)
                    if tail:
                        dve.wait_ge(h0_ready, b)
                    link(nc.vector.tensor_tensor(newt[v_], root[v_], root[v_], ALU.mult))
                    link(nc.vector.tensor_tensor(newt[v_], newt[v_], val[v_], ALU.mult))
                    link(nc.vector.tensor_scalar(newt[v_], newt[v_], -0.5, 1.5, ALU.mult, ALU.add))
                    link(nc.vector.tensor_tensor(rs[v_], root[v_], newt[v_], ALU.mult))
                    if tail:
                        link(nc.vector.tensor_tensor(x1d[0:P, C * F:], rs[0:P, 2 * C:], nonzero[0:P], ALU.mult))
                    nc.vector.tensor_tensor(shift[s_], neg_mean[s_], rs[s_], ALU.mult).then_inc(norm_ready, 1)
                    assert links[1] == (LINKS1 if tail else FIRST_LINKS), links

            def tail1(n, pos, ph):
                links[0] = FIRST_LINKS + n * LINKS1
                if pos == 1:
                    links[1] = 0
                    dve.wait_ge(chunk_used, ph.chunks(n, K - 1))
                    dve.wait_ge(first_half_saved, n + 1)
                    nc.vector.tensor_tensor(s_t[:], halves[1][:, 0:R], first_half[:], ALU.add).then_inc(s_ready, 1)
                if pos == 7:
                    dve.wait_ge(row_sums_ready, n + 1)
                    link(nc.vector.tensor_copy(sums_sb[0:P], sums_ps[0:P, 0:C]))
                    dve.wait_ge(nat_ready, n + 1)
                    for c in range(C):
                        ins = nc.vector.scalar_tensor_tensor(tmp[0:P, c], bi_sb[0:P], sums_sb[0:P, c:c + 1],
                                                             nat[0:P, c * F:(c + 1) * F], ALU.mult, ALU.add)
                    ins.then_inc(nat_read, 1)
                    dve.wait_ge(nat_read, n + 1)
                    link(nc.vector.tensor_tensor(tmp[0:P], tmp[0:P], bu_sb[0:P].unsqueeze(1).to_broadcast([P, C, F]),
                                                 ALU.add))
                    nc.vector.scalar_tensor_tensor(
                        x1d[0:P, 0:C * F], tmp[0:P].rearrange("p c f -> p (c f)"), 0.0,
                        x_in[0:P, 0:C * F], ALU.max, ALU.add).then_inc(x_used, 1)
                if pos == K - 1:
                    dve.wait_ge(x1_stored, 16 * (n + 1))
                    dve.wait_ge(h2s_ready, n + 1)

            def tail2(n, pos, ph, last):
                links[0] = FIRST_LINKS + NB * LINKS1 + (n if ph is CC else EARLY + (n - EARLY) * LINKS2)
                if pos == 1:
                    links[1] = 0
                    dve.wait_ge(chunk_used, ph.chunks(n, len(ph.order) - 1))
                    dve.wait_ge(first_half_saved, NB + n + 1)
                    ins = nc.vector.tensor_tensor(s_t[:], halves[1][:, 0:R], first_half[:], ALU.add)
                    if ph is D:
                        link(ins)
                        dve.wait_ge(part_loaded, 16 * (n - EARLY + 1))
                        ins = nc.vector.tensor_tensor(s_t[:], s_t[:], part[:], ALU.add)
                    ins.then_inc(s_ready, 1)
                if pos == 2:
                    dve.wait_ge(x1_loaded, 16 * (n + 1))
                    link(nc.vector.tensor_tensor(tmp[0:P], x_in[0:P, 0:C * F].rearrange("p (c f) -> p c f", c=C),
                                                 bl_sb[0:P].unsqueeze(1).to_broadcast([P, C, F]), ALU.add))
                if pos == 6:
                    dve.wait_ge(nat_ready, NB + n + 1)
                    for c in range(C):
                        ins = nc.vector.scalar_tensor_tensor(
                            res[0:P, c], nat[0:P, c * F:(c + 1) * F], x_in[0:P, C * F + c:C * F + c + 1],
                            tmp[0:P, c], ALU.mult, ALU.add)
                    ins.then_inc(res_ready, 1)
                if pos == last:
                    dve.wait_ge(out_stored, 16 * (n + 1))
                    assert links[1] == (1 if ph is CC else LINKS2), links

            def stream(ph, b, first):
                last = len(ph.order) - 1
                for pos in range(-1, last + 1):
                    if pos >= 0 and ph.split[pos]:
                        split_chunk(ph, b, pos)
                    if first:
                        for job in JOBS[ph.name]:
                            if job.pos == pos + 1 and not job.native:
                                split_features(job)
                    if ph.p == 1 and pos >= 0:
                        sum_chunk(ph, b, pos)
                    if pos >= 0 and tails(ph, b):
                        p, n, before = tails(ph, b)
                        if p == 1:
                            tail1(n, pos, before)
                        else:
                            tail2(n, pos, before, last)
                    if ph.p == 1 or ph is CC and first:
                        norms(all_blocks(ph, b), pos, ph.p == 1, bool(tails(ph, b)))
                    if ph is A and first and pos == last:
                        dve.wait_ge(consts_loaded, 16 * 6)

            nc.vector.memset(x1d[:], 0.0).then_inc(cleared, 1)
            nc.vector.memset(res[:], 0.0).then_inc(cleared, 1)
            dve.wait_ge(cleared, 2)
            run_phases(dve, stream)
            for pos in range(K):
                tail2(NB - 1, pos, D, K - 1)

        @block.tensor
        def _(pe):
            def multiply(ph, b, pos, first):
                k, half = ph.order[pos], len(ph.order) // 2
                within = pos % half
                made = [(halves[pos // half][:, 0:R], feature_slot(ph.p, k), within == 0, within == half - 1)]
                if ph is B and k < EARLY:
                    made.append((part_ps[:, 0:R], feature_slot(2, k), k == 0, k == EARLY - 1))
                if first:
                    jobs = [j for j in JOBS[ph.name] if j.pos == pos]
                    for j in jobs:
                        if j.native:
                            pe.wait_ge(native_loaded[j.slot], 16)
                        elif j is jobs[-1] or jobs[-1].native:
                            pe.wait_ge(feat_lo_ready, j.number + 1)
                buf = raw[0:P, pos % ph.raw]
                if not ph.split[pos]:
                    pe.wait_ge(raw_loaded[pos % ph.raw], 16 * ph.loads(b, pos))
                    for bank, slot, opens, closes in made:
                        for t in range(C):
                            last = nc.tensor.matmul(bank, feat_f32[0:P, slot, t], buf[:, t],
                                                    start=opens and t == 0, stop=closes and t == C - 1)
                    last.then_inc(chunk_used, 1)
                    return
                s = ph.split_slot(pos)
                pe.wait_ge(a_hi_ready, ph.splits(b, pos))
                for bank, slot, opens, closes in made:
                    for t in range(C):
                        nc.tensor.matmul(bank, feat_lo[0:P, slot, t], a_hi[0:P, s, t], start=opens and t == 0,
                                         stop=False)
                        last = nc.tensor.matmul(bank, feat_hi[0:P, slot, t], a_hi[0:P, s, t], start=False, stop=False)
                last.then_inc(a_hi_used, 1)
                pe.wait_ge(a_lo_ready, ph.splits(b, pos))
                for bank, slot, opens, closes in made:
                    for t in range(C):
                        last = nc.tensor.matmul(bank, feat_hi[0:P, slot, t], a_lo[0:P, s, t], start=False,
                                                stop=closes and t == C - 1)
                last.then_inc(chunk_used, 1)

            def row_sums(n):
                pe.wait_ge(rows_summed, n + 1)
                for c in range(C):
                    last = nc.tensor.matmul(sums_ps[0:P, c:c + 1], total[0:P, c * P:(c + 1) * P], ones[0:P],
                                            start=True, stop=True)
                last.then_inc(row_sums_ready, 1)

            def tail1(n, pos):
                if pos == 1:
                    row_sums(n)
                if pos == 4:
                    pe.wait_ge(s_ready, n + 1)
                    pe.wait_ge(h0_t_ready, n + 1)
                    for c in range(C):
                        nc.tensor.matmul(nat[0:P, c * F:(c + 1) * F], s_t[:, c * P:(c + 1) * P], wi_sb[:],
                                         start=True, stop=False)
                        last = nc.tensor.matmul(nat[0:P, c * F:(c + 1) * F], h0_t[:, c * P:(c + 1) * P], wu_sb[:],
                                                start=False, stop=True)
                    last.then_inc(nat_ready, 1)

            def user_part(n, pos):
                if pos == 16:
                    pe.wait_ge(h0_ready, n + 1)
                    for c in range(C):
                        last = nc.tensor.transpose(h0_ps[:, c * P:(c + 1) * P], h0[0:P, c], ident[0:P, 0:P])
                    last.then_inc(h0_turned, 1)

            def tail2(n, pos):
                if pos == 3:
                    pe.wait_ge(s_ready, NB + n + 1)
                    for c in range(C):
                        last = nc.tensor.matmul(nat[0:P, c * F:(c + 1) * F], s_t[:, c * P:(c + 1) * P], w_sb[:],
                                                start=True, stop=True)
                    last.then_inc(nat_ready, 1)

            def stream(ph, b, first):
                half = len(ph.order) // 2
                for pos in range(len(ph.order)):
                    if pos == 0 and tails(ph, b):
                        pe.wait_ge(first_half_saved, all_blocks(ph, b))
                    if pos == half and tails(ph, b):
                        pe.wait_ge(s_ready, all_blocks(ph, b))
                    if ph is B and not first and ph.order[pos] == 0:
                        pe.wait_ge(part_saved, b - EARLY)
                    multiply(ph, b, pos, first)
                    if tails(ph, b):
                        p, n, before = tails(ph, b)
                        if p == 1:
                            tail1(n, pos)
                        else:
                            tail2(n, pos)
                    if ph.p == 1:
                        user_part(b, pos)
                    if ph is A and first and pos == len(ph.order) - 1:
                        pe.wait_ge(consts_loaded, 16 * 6)

            pe.wait_ge(ident_ready, 2)
            pe.wait_ge(ones_ready, 1)
            run_phases(pe, stream)
            for pos in range(K):
                tail2(NB - 1, pos)


def kernel(x, adj, L0_gnn_item_feat, L0_gnn_W_item, L0_gnn_b_item, L0_gnn_W_user, L0_gnn_b_user, L1_gnn_W, L1_gnn_b):
    import numpy as np
    import concourse.bacc as bacc
    from concourse.bass_utils import run_bass_kernel_spmd

    def rows(a):
        a = np.asarray(a)
        padded = np.zeros((NB, 128, C, F), a.dtype)
        padded[:, :P] = a.reshape(NB, C, P, F).transpose(0, 2, 1, 3)
        return padded

    def columns(a):
        return np.ascontiguousarray(np.asarray(a).T)

    def on_all(a):
        return np.ascontiguousarray(np.broadcast_to(np.asarray(a), (128, F)))

    a = np.asarray(adj).reshape(NB, R, K, C, P)
    blocks = np.zeros((NB, K, 128, C, R), a.dtype)
    for b in range(NB):
        blocks[b, :, :P] = a[b].transpose(1, 3, 2, 0)
    arrays = {
        "adj": blocks, "items": rows(L0_gnn_item_feat), "xs": rows(x),
        "wi": columns(L0_gnn_W_item), "wu": columns(L0_gnn_W_user), "w": columns(L1_gnn_W),
        "bi": on_all(L0_gnn_b_item), "bu": on_all(L0_gnn_b_user), "bl": on_all(L1_gnn_b),
    }
    nc = bacc.Bacc("TRN2", target_bir_lowering=False, num_devices=1)
    ins = [nc.dram_tensor(n, v.shape, mybir.dt.float32, kind="ExternalInput").ap() for n, v in arrays.items()]
    out = nc.dram_tensor("out", (NB, 128, C, F), mybir.dt.float32, kind="ExternalOutput").ap()
    gnn_kernel(nc, *ins, out)
    got = run_bass_kernel_spmd(nc, [arrays], core_ids=[0]).results[0]["out"]
    return np.ascontiguousarray(np.asarray(got).reshape(NB, 128, C, F)[:, :P].transpose(0, 2, 1, 3)).reshape(N, F)
```
